# Optimizing a Trainium2 kernel written in Bass

```python
import numpy as np
import jax
import jax.numpy as jnp

def _softmax(x, axis=-1):
    return jax.nn.softmax(x, axis=axis)

def _gelu(x):
    return jax.nn.gelu(x, approximate=True)

def _silu(x):
    return jax.nn.silu(x)

def _sigmoid(x):
    return jax.nn.sigmoid(x)

def _layernorm(x, axis=-1, eps=1e-05):
    m = jnp.mean(x, axis=axis, keepdims=True)
    v = jnp.var(x, axis=axis, keepdims=True)
    return (x - m) / jnp.sqrt(v + eps)

def _scatter_add(tgt, idx, src, axis=0):
    return tgt.at[idx].add(src)

def _segment_sum(src, seg, n):
    return jax.ops.segment_sum(src, seg, n)
kernel_name = 'mk_flamingo_gated_d1_seqx_r2_6e531b'

def setup_inputs(seed: int=0):
    np.random.seed(seed)
    _w = jnp.asarray

    def _rec_inputs():
        import jax
        import jax.numpy as jnp
        _rk = jax.random.key(seed)
        x = 7.22e-05 + 1 * jax.random.normal(jax.random.fold_in(_rk, 1), (8, 1024, 512), jnp.float32)
        _lenS = 1024 - jax.random.randint(jax.random.fold_in(_rk, 7), (8,), 0, max(1, 1024 // 4) + 1, jnp.int32)
        _lenS2 = 1024 - jax.random.randint(jax.random.fold_in(_rk, 8), (8,), 0, max(1, 1024 // 4) + 1, jnp.int32)
        _ctx_1024P = jax.random.normal(jax.random.fold_in(_rk, 11), (8, 16, 512), jnp.float32)
        _ctx_1024c = jax.random.dirichlet(jax.random.fold_in(_rk, 511), 0.3 * jnp.ones((16,), jnp.float32), (8, 1024))
        _ctx_1024t = jnp.einsum('bsk,bkd->bsd', _ctx_1024c, _ctx_1024P)
        _ctx_1024t = _ctx_1024t * jax.lax.rsqrt(jnp.mean(jnp.square(_ctx_1024t)) + 1e-12) * 0.953939
        ctx_1024 = 4.13588e-05 + 0.999923 * (_ctx_1024t + 0.3 * jax.random.normal(jax.random.fold_in(_rk, 611), (8, 1024, 512), jnp.float32))
        _validS = jnp.arange(1024)[None, :] < _lenS[:, None]
        _validS2 = jnp.arange(1024)[None, :] < _lenS2[:, None]
        _causal = jnp.tril(jnp.ones((1024, 1024), dtype=bool))
        mask_1xSxS2_ff0 = jnp.where(jnp.ones((1, 1024, 1024), dtype=bool), 0.0, -1000000000.0).astype(jnp.float32)
        _g = jax.random.normal(jax.random.fold_in(_rk, 9001), (2, 1), jnp.float32)
        _g = jnp.sign(_g) * jnp.maximum(jnp.abs(_g), 1.0) + (_g == 0) * 1.0
        g_xattn = _g[0]
        g_ffn = _g[1]
        return (x, ctx_1024, mask_1xSxS2_ff0, g_xattn, g_ffn)
    x, ctx_1024, mask_1xSxS2_ff0, g_xattn, g_ffn = _rec_inputs()

    def _L0_xattn_setup():
        import jax, jax.numpy as jnp
        import numpy as np
        B, S, D_IN, D_MODEL = (4, 1024, 512, 512)
        key = jax.random.key(seed)
        ks = jax.random.split(key, 8)
        glorot = np.sqrt(6.0 / (D_IN + D_MODEL))
        inp = {'q': jax.random.normal(ks[0], (B, S, D_IN), dtype=jnp.float32), 'k': jax.random.normal(ks[1], (B, S, D_IN), dtype=jnp.float32), 'v': jax.random.normal(ks[2], (B, S, D_IN), dtype=jnp.float32), 'mask': jnp.zeros((1, S, S), dtype=jnp.float32), 'kernel_q': jax.random.uniform(ks[3], (1, 1, D_IN, D_MODEL), jnp.float32, -glorot, glorot), 'kernel_k': jax.random.uniform(ks[4], (1, 1, D_IN, D_MODEL), jnp.float32, -glorot, glorot), 'kernel_v': jax.random.uniform(ks[5], (1, 1, D_IN, D_MODEL), jnp.float32, -glorot, glorot), 'bias_q': 0.05 * jax.random.normal(ks[6], (D_MODEL,), dtype=jnp.float32), 'bias_k': 0.05 * jax.random.normal(ks[7], (D_MODEL,), dtype=jnp.float32), 'bias_v': 0.05 * jax.random.normal(jax.random.fold_in(key, 7), (D_MODEL,), dtype=jnp.float32)}
        return inp
    _L0_xattn_all = _L0_xattn_setup()
    _L0_xattn_in = {k: v for k, v in _L0_xattn_all.items() if k in ('kernel_q', 'kernel_k', 'kernel_v', 'bias_q', 'bias_k', 'bias_v')}
    del _L0_xattn_all

    def _L0_ffn_setup():
        import jax, jax.numpy as jnp
        import numpy as np
        DIM = 512
        HIDDEN = 1536
        SCALE = 1.0 / 127.0

        def _dequant(w_int, dtype):
            return w_int.astype(dtype) * jnp.asarray(SCALE, dtype)
        key = jax.random.key(seed)
        k_x, k_g, k_u, k_d = jax.random.split(key, 4)
        x = jax.random.normal(k_x, (4, 1024, DIM), dtype=jnp.float32)
        w_gate = jax.random.randint(k_g, (HIDDEN, DIM), -127, 128, dtype=jnp.int32)
        w_up = jax.random.randint(k_u, (HIDDEN, DIM), -127, 128, dtype=jnp.int32)
        w_down = jax.random.randint(k_d, (DIM, HIDDEN), -127, 128, dtype=jnp.int32)
        return {'x': x, 'w_gate': w_gate, 'w_up': w_up, 'w_down': w_down}
    _L0_ffn_all = _L0_ffn_setup()
    _L0_ffn_in = {k: v for k, v in _L0_ffn_all.items() if k in ('w_gate', 'w_up', 'w_down')}
    del _L0_ffn_all
    return {'x': x, 'ctx_1024': ctx_1024, 'mask_1xSxS2_ff0': mask_1xSxS2_ff0, 'g_xattn': g_xattn, 'g_ffn': g_ffn, 'L0_xattn_kernel_q': _L0_xattn_in['kernel_q'], 'L0_xattn_kernel_k': _L0_xattn_in['kernel_k'], 'L0_xattn_kernel_v': _L0_xattn_in['kernel_v'], 'L0_xattn_bias_q': _L0_xattn_in['bias_q'], 'L0_xattn_bias_k': _L0_xattn_in['bias_k'], 'L0_xattn_bias_v': _L0_xattn_in['bias_v'], 'L0_ffn_w_gate': _L0_ffn_in['w_gate'], 'L0_ffn_w_up': _L0_ffn_in['w_up'], 'L0_ffn_w_down': _L0_ffn_in['w_down']}

def reference(x, ctx_1024, mask_1xSxS2_ff0, g_xattn, g_ffn, L0_xattn_kernel_q, L0_xattn_kernel_k, L0_xattn_kernel_v, L0_xattn_bias_q, L0_xattn_bias_k, L0_xattn_bias_v, L0_ffn_w_gate, L0_ffn_w_up, L0_ffn_w_down):
    import jax
    import jax.numpy as jnp

    def _L0_xattn_ref(q, k, v, mask, kernel_q, kernel_k, kernel_v, bias_q, bias_k, bias_v):
        import jax, jax.numpy as jnp
        import numpy as np
        B, S, D_IN, D_MODEL = (4, 1024, 512, 512)
        Wq, Wk, Wv = (kernel_q[0, 0], kernel_k[0, 0], kernel_v[0, 0])
        qp = jax.nn.relu(jnp.einsum('bsd,de->bse', q, Wq) + bias_q)
        kp = jax.nn.relu(jnp.einsum('bsd,de->bse', k, Wk) + bias_k)
        vp = jax.nn.relu(jnp.einsum('bsd,de->bse', v, Wv) + bias_v)
        scores = jax.nn.relu(jnp.einsum('bqe,bke->bqk', qp, kp))
        dk = jnp.asarray(kp.shape[-1], dtype=scores.dtype)
        logits = scores / jnp.sqrt(dk) + mask
        out = jax.nn.relu(jnp.einsum('bqk,bke->bqe', logits, vp))
        return out

    def _L0_ffn_ref(x, w_gate, w_up, w_down):
        import jax, jax.numpy as jnp
        import numpy as np
        DIM = 512
        HIDDEN = 1536
        SCALE = 1.0 / 127.0

        def _dequant(w_int, dtype):
            return w_int.astype(dtype) * jnp.asarray(SCALE, dtype)
        wg = _dequant(w_gate, x.dtype)
        wu = _dequant(w_up, x.dtype)
        wd = _dequant(w_down, x.dtype)
        gate = jnp.einsum('bsd,hd->bsh', x, wg)
        up = jnp.einsum('bsd,hd->bsh', x, wu)
        h = jax.nn.silu(gate) * up
        return jnp.einsum('bsh,dh->bsd', h, wd)
    x = x + jnp.tanh(g_xattn[0]) * _L0_xattn_ref(_layernorm(x, axis=-1), ctx_1024, ctx_1024, mask_1xSxS2_ff0, L0_xattn_kernel_q, L0_xattn_kernel_k, L0_xattn_kernel_v, L0_xattn_bias_q, L0_xattn_bias_k, L0_xattn_bias_v)
    x = x + jnp.tanh(g_ffn[0]) * _L0_ffn_ref(_layernorm(x, axis=-1), L0_ffn_w_gate, L0_ffn_w_up, L0_ffn_w_down)
    return x

_drawn_inputs = setup_inputs


def setup_inputs(seed=0):
    import zlib

    import numpy as np

    out = dict(_drawn_inputs(seed))
    spreads = {}
    factors = {'L0_xattn_bias_q': 8.0, 'L0_xattn_bias_k': 21.714}
    for name, (base, spread) in spreads.items():
        noise = np.random.default_rng([zlib.crc32(name.encode()), seed]).standard_normal(out[name].shape)
        drawn = base * np.exp(spread * noise) if base else spread * noise
        out[name] = jnp.asarray(drawn.astype(out[name].dtype))
    for name, factor in factors.items():
        out[name] = (out[name] * factor).astype(out[name].dtype)
    return out
```

```python
import numpy as np
from contextlib import ExitStack
import concourse.bass as bass
from concourse import mybir


def build(nc, x, ctx_t, mask_t, g_xattn, g_ffn, w_q, w_k, w_v, b_q, b_k, b_v, wg_t, wu_t, wd_t, out, x2):
    f32, f32r, i32 = mybir.dt.float32, mybir.dt.float32r, mybir.dt.int32
    ALU = mybir.AluOpType
    ACT = mybir.ActivationFunctionType

    B, S, D = x.shape
    H = wg_t.shape[1]
    P = 128
    NT = 512
    DC, HC = D // P, H // P
    KT = S // P
    UNITS = S // NT
    TILES = NT // P
    BLOCKS = B * UNITS
    SCORE_SCALE = float(D) ** -0.5
    DEQUANT = 1.0 / 127.0
    EPS = 1e-5
    BANKS = 4
    LAG = 2
    PROBS = LAG + 1
    assert UNITS == 2 and TILES == DC == BANKS == 4

    order = ([("k", 0, e) for e in range(DC)] + [("v", t) for t in (0, 1)] + [("t", 0, j) for j in range(TILES)]
             + [("v", t) for t in (2, 3)] + [("q", 0, e) for e in range(DC)] + [("k", 1, e) for e in range(DC)]
             + [("v", t) for t in range(4, 8)] + [("s", 0, k) for k in range(5)] + [("t", 1, j) for j in range(TILES)]
             + [("s", 0, k) for k in range(5, KT)] + [("q", 1, e) for e in range(DC)] + [("s", 1, k) for k in range(KT)])
    G = len(order)
    assert G % BANKS == 0
    gid = {name: n for n, name in enumerate(order)}
    by_act = [name for name in order if name[0] in "kq"]
    by_dve = [name for name in order if name[0] in "vs"]
    aid = {name: n for n, name in enumerate(by_act)}
    vid = {name: n for n, name in enumerate(by_dve)}
    NA, NV = len(by_act), len(by_dve)

    es = ExitStack()
    with es:
        def sb(name, shape, dt=f32):
            return es.enter_context(nc.sbuf_tensor(name, shape, dt))

        def sem(name):
            return es.enter_context(nc.semaphore(name))

        OPW = DC * D
        operands = sb("operands", [P, 10 * OPW], f32r)

        def operand(n):
            return operands[:, n * OPW:(n + 1) * OPW].rearrange("p (c n) -> p c n", c=DC)
        wk_hi, wk_lo, wv_hi, wv_lo, ctx_hi, ctx_lo, wq_hi, wq_lo, z_hi, z_lo = (operand(n) for n in range(10))
        ffn_gate = operands[:, 0:DC * H].rearrange("p (c n) -> p c n", c=DC)
        ffn_up = operands[:, DC * H:2 * DC * H].rearrange("p (c n) -> p c n", c=DC)
        ffn_down = operands[:, 2 * DC * H:2 * DC * H + HC * D].rearrange("p (c n) -> p c n", c=HC)
        assert 2 * DC * H == 6 * OPW

        AW = DC * NT
        acts = sb("acts", [P, (2 + 4 + 4) * AW + PROBS * 2 * NT], f32r)
        qp = [acts[:, n * AW:(n + 1) * AW].rearrange("p (c n) -> p c n", c=DC) for n in (0, 1)]
        kp = [acts[:, (2 + 2 * n) * AW:(4 + 2 * n) * AW].rearrange("p (c n) -> p c n", c=DC) for n in (0, 1)]
        vp = [acts[:, (6 + 2 * n) * AW:(8 + 2 * n) * AW].rearrange("p (c n) -> p c n", c=KT) for n in (0, 1)]
        pr0 = 10 * AW
        probs = [[acts[:, pr0 + (2 * s + n) * NT:pr0 + (2 * s + n + 1) * NT] for n in (0, 1)] for s in range(PROBS)]
        z2_hi, z2_lo = qp
        hid = [acts[:, 2 * AW + n * HC * NT:2 * AW + (n + 1) * HC * NT].rearrange("p (c n) -> p c n", c=HC)
               for n in (0, 1)]

        raw = sb("raw", [P, 2, NT])
        x_in = sb("x_in", [P, TILES, D])
        x_res = sb("x_res", [P, TILES, D])
        mask = sb("mask", [P, 2, NT])
        staged = sb("staged", [P, BANKS, NT])
        bv = sb("bv", [P, D])
        bqk = sb("bqk", [P, 2, DC])
        bqs = sb("bqs", [P, DC])
        ident = sb("ident", [P, P])
        eps = sb("eps", [P, 1])
        gates = sb("gates", [P, 2])
        tg = sb("tg", [P, 2])
        tg_ffn = sb("tg_ffn", [P, 1])
        bn = sb("bn", [P, TILES, 6])
        mv = sb("mv", [P, TILES, 2])
        std = sb("std", [P, TILES])
        rstd = sb("rstd", [P, TILES])

        bank = [es.enter_context(nc.psum_tensor(f"bank{n}", [P, NT], f32)) for n in range(BANKS)]
        acc = [es.enter_context(nc.psum_tensor(f"acc{n}", [P, D], f32)) for n in range(TILES)]

        carrier = sem("carrier")
        small_loaded = sem("small_loaded")
        w_loaded = [sem(f"w_loaded{n}") for n in range(8)]
        w_hi_done, w_split = sem("w_hi_done"), sem("w_split")
        ident_set = sem("ident_set")
        consts_set, consts_ready = sem("consts_set"), sem("consts_ready")
        raw_loaded = [sem(f"raw_loaded{n}") for n in (0, 1)]
        ctx_hi_done, ctx_split = sem("ctx_hi_done"), sem("ctx_split")
        x_loaded = [sem(f"x_loaded{n}") for n in range(TILES)]
        res_loaded = [sem(f"res_loaded{n}") for n in range(TILES)]
        stored = [sem(f"stored{n}") for n in range(TILES)]
        mask_loaded = [sem(f"mask_loaded{n}") for n in (0, 1)]
        bn_done, mv_done, std_done, rstd_done, z_ready = (sem(n) for n in
                                                          ("bn_done", "mv_done", "std_done", "rstd_done", "z_ready"))
        group_ready = sem("group_ready")
        staged_act, staged_dve = sem("staged_act"), sem("staged_dve")
        hi_done = sem("hi_done")
        split_done = sem("split_done")
        acc_ready, relu_done = sem("acc_ready"), sem("relu_done")
        x2_ready = sem("x2_ready")
        ffn_cast = sem("ffn_cast")
        ffn_ready = sem("ffn_ready")
        z2_hi_done, z2_split = sem("z2_hi_done"), sem("z2_split")
        silu_done, hid_full, hid_hi_done, hid_split = (sem(n) for n in ("silu_done", "hid_full", "hid_hi_done", "hid_split"))
        down_ready, y_ready = sem("down_ready"), sem("y_ready")

        def split_at(b, name):
            return b * G + gid[name] + 1 + BANKS

        def free_at(b, name):
            return b * G + gid[name] + 1

        LAST = B - 1
        W_PIECES = 3 * DC
        FFN_PIECES = 3 * HC
        CTX_PIECES = UNITS * DC
        RAW_CTX = B * CTX_PIECES
        LN_A = B * UNITS

        def w_piece(n):
            w, c = (w_k, w_v, w_q)[n // DC], n % DC
            hi, lo = ((wk_hi, wk_lo), (wv_hi, wv_lo), (wq_hi, wq_lo))[n // DC]
            return w[c * P:(c + 1) * P, :], n % 8, hi[:, c, :], lo[:, c, :]

        def w_slot(s):
            return staged[:, s, :] if s < 4 else x_res[:, s - 4, :]

        def ffn_piece(n):
            kind, m = divmod(n, HC)
            if kind < 2:
                c, h = divmod(m, H // NT)
                src = (wg_t, wu_t)[kind][c * P:(c + 1) * P, h * NT:(h + 1) * NT]
                return src, (ffn_gate, ffn_up)[kind][:, c, h * NT:(h + 1) * NT]
            return wd_t[m * P:(m + 1) * P, :], ffn_down[:, m, :]

        block = es.enter_context(nc.Block())

        @block.sync
        def _(sp):
            def sp_wait(semaphore, value):
                sp.wait_ge(semaphore, value)
                sp.sem_inc(carrier, 1)

            def load_w(n):
                src, s, _, _ = w_piece(n)
                if n >= 8:
                    sp.wait_ge(w_split, n - 7)
                sp.dma_start(w_slot(s), src).then_inc(w_loaded[s], 16)

            def load_ctx(b, blk, c):
                n = blk * DC + c
                if not (isinstance(b, int) and b == 0 and n < 2):
                    sp_wait(ctx_split, b * CTX_PIECES + n - 1)
                sp.dma_start(raw[:, n % 2, :], ctx_t[b, c * P:(c + 1) * P, blk * NT:(blk + 1) * NT]) \
                    .then_inc(raw_loaded[n % 2], 16)

            def load_x(b, u, j):
                r = u * NT + j * P
                sp.dma_start(x_in[:, j, :], x[b, r:r + P, :]).then_inc(x_loaded[j], 16)

            def load_res(b, u, j):
                r = u * NT + j * P
                sp.dma_start(x_res[:, j, :], x[b, r:r + P, :]).then_inc(res_loaded[j], 16)

            def store_x2(b, u):
                for j in range(TILES):
                    r = u * NT + j * P
                    sp_wait(x2_ready, TILES * (b * UNITS + u + 1) + j + 1)
                    sp.dma_start(x2[b, r:r + P, :], x_res[:, j, :]).then_inc(stored[j], 16)

            def load_ffn(n):
                if n < 2:
                    sp.wait_ge(ctx_split, RAW_CTX - 1 + n)
                else:
                    sp.wait_ge(ffn_cast, n - 1)
                sp.dma_start(raw[:, n % 2, :].bitcast(i32), ffn_piece(n)[0]).then_inc(raw_loaded[n % 2], 16)

            for n in range(4):
                load_w(n)
            for c in range(2):
                load_ctx(0, 0, c)
            for n in range(4, 8):
                load_w(n)
            for j in range(TILES):
                load_x(0, 0, j)
            for c in range(2, DC):
                load_ctx(0, 0, c)
            for n in range(8, W_PIECES):
                load_w(n)
            sp.wait_ge(w_split, W_PIECES)
            for j in range(TILES):
                load_res(0, 0, j)

            def batch(b, last):
                for j in range(TILES):
                    sp_wait(group_ready, b * G + gid["t", 0, j] + 1)
                    load_x(b, 1, j)
                for c in range(DC):
                    load_ctx(b, 1, c)
                if last:
                    for n in range(15):
                        load_ffn(n)
                for j in range(TILES):
                    sp_wait(group_ready, b * G + gid["t", 1, j] + 1)
                    if last:
                        sp.dma_start(x_in[:, j, :], x2[0, j * P:(j + 1) * P, :]).then_inc(x_loaded[j], 16)
                    else:
                        load_x(b + 1, 0, j)
                if last:
                    for n in range(15, HC * 2):
                        load_ffn(n)
                else:
                    for c in range(2):
                        load_ctx(b + 1, 0, c)
                store_x2(b, 0)
                for j in range(TILES):
                    sp_wait(stored[j], 16 * (b * UNITS + 1))
                    load_res(b, 1, j)
                if last:
                    for n in range(HC * 2, FFN_PIECES):
                        load_ffn(n)
                else:
                    for c in range(2, DC):
                        load_ctx(b + 1, 0, c)
                store_x2(b, 1)
                if not last:
                    for j in range(TILES):
                        sp_wait(stored[j], 16 * (b * UNITS + 2))
                        load_res(b + 1, 0, j)

            with sp.Fori(0, LAST) as b:
                batch(b, False)
            batch(LAST, True)

            for j in range(TILES):
                sp.wait_ge(stored[j], 16 * BLOCKS)
            x2_rows = x2.rearrange("b (t n) d -> (b t) n d", n=NT)
            out_rows = out.rearrange("b (t n) d -> (b t) n d", n=NT)

            def ffn_block(t, last):
                for j in range(TILES):
                    sp_wait(stored[j], 16 * (BLOCKS + t))
                    sp.dma_start(x_res[:, j, :], x2_rows[t, j * P:(j + 1) * P, :]).then_inc(res_loaded[j], 16)
                if not last:
                    for j in range(TILES):
                        sp_wait(ffn_ready, TILES + t * (2 * HC + TILES) - TILES + j + 1)
                        sp.dma_start(x_in[:, j, :], x2_rows[t + 1, j * P:(j + 1) * P, :]).then_inc(x_loaded[j], 16)
                for j in range(TILES):
                    sp_wait(y_ready, TILES * t + j + 1)
                    sp.dma_start(out_rows[t, j * P:(j + 1) * P, :], x_res[:, j, :]).then_inc(stored[j], 16)

            with sp.Fori(0, BLOCKS - 1) as t:
                ffn_block(t, False)
            ffn_block(BLOCKS - 1, True)
            for j in range(TILES):
                sp.wait_ge(stored[j], 16 * 2 * BLOCKS)

        @block.gpsimd
        def _(pool):
            pool.dma_start(bqk[:, 0, :], b_q).then_inc(small_loaded, 16)
            pool.dma_start(bqk[:, 1, :], b_k).then_inc(small_loaded, 16)
            pool.dma_start(bv[:, :], b_v.rearrange("(a n) -> a n", a=1).to_broadcast([P, D])).then_inc(small_loaded, 16)
            pool.dma_start(gates[:, 0:1], g_xattn.rearrange("(a n) -> a n", a=1).to_broadcast([P, 1])) \
                .then_inc(small_loaded, 16)
            pool.dma_start(gates[:, 1:2], g_ffn.rearrange("(a n) -> a n", a=1).to_broadcast([P, 1])) \
                .then_inc(small_loaded, 16)
            pool.memset(ident[:, :], 0.0).then_inc(ident_set, 1)
            pool.wait_ge(ident_set, 1)
            pool.affine_select(out=ident[:, :], in_=ident[:, :], compare_op=ALU.not_equal, fill=1.0, base=0,
                               pattern=[[-1, P]], channel_multiplier=1).then_inc(ident_set, 1)
            with pool.Fori(0, B) as b:
                for m in range(UNITS * KT):
                    u, k = divmod(m, KT)
                    before = by_dve[vid["s", *divmod(m - 2, KT)]] if m >= 2 else by_dve[0]
                    pool.wait_ge(staged_dve, b * NV + vid[before] + 1)
                    pool.sem_inc(carrier, 1)
                    pool.dma_start(mask[:, m % 2, :], mask_t[k * P:(k + 1) * P, u * NT:(u + 1) * NT]) \
                        .then_inc(mask_loaded[m % 2], 16)

        @block.scalar
        def _(act):
            act.wait_ge(small_loaded, 16 * 5)
            nc.scalar.activation(tg[:, :], gates[:, :], ACT.Tanh).then_inc(consts_ready, 1)
            nc.scalar.activation(bqs[:, :], bqk[:, 0, :], ACT.Copy, scale=SCORE_SCALE).then_inc(consts_ready, 1)
            act.wait_ge(consts_ready, 2)

            def w_hi(n):
                _, s, hi, _ = w_piece(n)
                act.wait_ge(w_loaded[s], 16 * (n // 8 + 1))
                nc.scalar.activation(hi, w_slot(s), ACT.Copy).then_inc(w_hi_done, 1)

            def ctx_part(b, blk, c):
                n = blk * DC + c
                act.wait_ge(raw_loaded[n % 2], 16 * (b * (CTX_PIECES // 2) + n // 2 + 1))
                nc.scalar.activation(ctx_hi[:, c, :], raw[:, n % 2, :], ACT.Copy).then_inc(ctx_hi_done, 1)

            def ffn_weights(n):
                act.wait_ge(raw_loaded[n % 2], 16 * ((RAW_CTX + n) // 2 + 1))
                nc.scalar.activation(ffn_piece(n)[1], raw[:, n % 2, :].bitcast(i32), ACT.Copy).then_inc(ffn_cast, 1)

            def project(b, name):
                g = gid[name]
                kind, blk, e = name
                act.wait_ge(group_ready, b * G + g + 1)
                act.wait_ge(split_done, free_at(b, name))
                bias, scale = (bqs[:, e:e + 1], SCORE_SCALE) if kind == "q" else (bqk[:, 1, e:e + 1], 1.0)
                nc.scalar.activation(staged[:, g % BANKS, :], bank[g % BANKS][:, :], ACT.Relu, bias=bias,
                                     scale=scale).then_inc(staged_act, 1)
                act.wait_ge(staged_act, b * NA + aid[name] + 1)
                dst = qp[0][:, e, :] if kind == "q" else kp[0][:, e, blk * NT:(blk + 1) * NT]
                nc.scalar.activation(dst, staged[:, g % BANKS, :], ACT.Copy).then_inc(hi_done, 1)

            def value(b, name):
                g = gid[name]
                act.wait_ge(staged_dve, b * NV + vid[name] + 1)
                nc.scalar.activation(vp[0][:, name[1], :], staged[:, g % BANKS, :], ACT.Relu).then_inc(hi_done, 1)

            def logits(b, name):
                g = gid[name]
                act.wait_ge(staged_dve, b * NV + vid[name] + 1)
                nc.scalar.activation(probs[name[2] % PROBS][0], staged[:, g % BANKS, :], ACT.Copy).then_inc(hi_done, 1)

            def transposed(b, name):
                g = gid[name]
                act.wait_ge(group_ready, b * G + g + 1)
                nc.scalar.activation(z_hi[:, :, name[2] * P:(name[2] + 1) * P],
                                     bank[g % BANKS][:, :].rearrange("p (c n) -> p c n", c=DC), ACT.Copy) \
                    .then_inc(hi_done, 1)

            def square_root(ln):
                act.wait_ge(mv_done, TILES * (ln + 1))
                nc.scalar.activation(std[:, :], mv[:, :, 1], ACT.Sqrt, bias=eps[:, 0:1]).then_inc(std_done, 1)

            def attended(b, u):
                for j in range(TILES):
                    act.wait_ge(acc_ready, TILES * (b * UNITS + u) + j + 1)
                    nc.scalar.activation(acc[j][:, :], acc[j][:, :], ACT.Relu).then_inc(relu_done, 1)

            for n in range(4):
                w_hi(n)
            ctx_part(0, 0, 0)
            ctx_part(0, 0, 1)
            for n in range(4, 8):
                w_hi(n)
            ctx_part(0, 0, 2)
            ctx_part(0, 0, 3)
            for n in range(8, W_PIECES):
                w_hi(n)
            act.wait_ge(consts_set, 1)
            act.wait_ge(w_split, W_PIECES)

            def batch(b, last):
                for e in range(DC):
                    project(b, ("k", 0, e))
                square_root(b * UNITS)
                for t in (0, 1):
                    value(b, ("v", t))
                for j in range(TILES):
                    transposed(b, ("t", 0, j))
                for t in (2, 3):
                    value(b, ("v", t))
                for e in range(DC):
                    ctx_part(b, 1, e)
                    project(b, ("q", 0, e))
                for e in range(DC):
                    project(b, ("k", 1, e))
                for t in range(4, 8):
                    value(b, ("v", t))
                for k in range(5):
                    logits(b, ("s", 0, k))
                    if k == 1:
                        square_root(b * UNITS + 1)
                    if last:
                        for n in range(3 * k, 3 * k + 3):
                            ffn_weights(n)
                for j in range(TILES):
                    transposed(b, ("t", 1, j))
                for k in range(5, KT):
                    logits(b, ("s", 0, k))
                    if last:
                        for n in range(3 * k, 3 * k + 3):
                            ffn_weights(n)
                for e in range(DC):
                    project(b, ("q", 1, e))
                attended(b, 0)
                for k in range(KT):
                    logits(b, ("s", 1, k))
                    if last and k < 6:
                        for n in range(2 * HC + 2 * k, 2 * HC + 2 * k + 2):
                            ffn_weights(n)
                    if last and k == 2:
                        square_root(LN_A)
                    if not last and k < DC:
                        ctx_part(b + 1, 0, k)
                if last:
                    z2_parts(0)
                attended(b, 1)

            def z2_parts(t):
                for j in range(TILES):
                    act.wait_ge(ffn_ready, t * (2 * HC + TILES) + j + 1)
                    nc.scalar.activation(z2_hi[:, :, j * P:(j + 1) * P],
                                         bank[j][:, :].rearrange("p (c n) -> p c n", c=DC), ACT.Copy) \
                        .then_inc(z2_hi_done, 1)

            with act.Fori(0, LAST) as b:
                batch(b, False)
            batch(LAST, True)

            def ffn_block(t, last):
                base = TILES + t * (2 * HC + TILES)
                for c in range(HC):
                    act.wait_ge(ffn_ready, base + 2 * c + 1)
                    if c >= BANKS:
                        act.wait_ge(hid_split, t * HC + c - BANKS + 1)
                    nc.scalar.activation(staged[:, c % BANKS, :], bank[2 * c % BANKS][:, :], ACT.Silu, scale=DEQUANT) \
                        .then_inc(silu_done, 1)
                    act.wait_ge(hid_full, t * HC + c + 1)
                    nc.scalar.activation(hid[0][:, c, :], staged[:, c % BANKS, :], ACT.Copy).then_inc(hid_hi_done, 1)
                if not last:
                    square_root(LN_A + 1 + t)
                    z2_parts(t + 1)

            with act.Fori(0, BLOCKS - 1) as t:
                ffn_block(t, False)
            ffn_block(BLOCKS - 1, True)

        @block.vector
        def _(dve):
            nc.vector.memset(eps[:, :], EPS).then_inc(consts_set, 1)
            dve.sem_inc(split_done, BANKS)
            dve.sem_inc(x2_ready, TILES)
            dve.wait_ge(consts_ready, 2)
            nc.vector.tensor_scalar(tg_ffn[:, :], tg[:, 1:2], DEQUANT, DEQUANT, ALU.mult, ALU.mult).then_inc(consts_set, 1)

            def w_lo(n):
                _, s, hi, lo = w_piece(n)
                dve.wait_ge(w_hi_done, n + 1)
                nc.vector.tensor_tensor(lo, w_slot(s), hi.bitcast(f32), ALU.subtract).then_inc(w_split, 1)

            def ctx_part(b, blk, c):
                n = blk * DC + c
                dve.wait_ge(ctx_hi_done, b * CTX_PIECES + n + 1)
                nc.vector.tensor_tensor(ctx_lo[:, c, :], raw[:, n % 2, :], ctx_hi[:, c, :].bitcast(f32), ALU.subtract) \
                    .then_inc(ctx_split, 1)

            def statistics(ln, j):
                dve.wait_ge(x_loaded[j], 16 * (ln + 1))
                nc.vector.bn_stats(bn[:, j, :], x_in[:, j, :]).then_inc(bn_done, 1)
                dve.wait_ge(bn_done, TILES * ln + j + 1)
                dve.sem_inc(carrier, 1)
                nc.vector.bn_aggr(mv[:, j, :], bn[:, j, :]).then_inc(mv_done, 1)

            def inverse(ln):
                dve.wait_ge(std_done, ln + 1)
                nc.vector.reciprocal(rstd[:, :], std[:, :]).then_inc(rstd_done, 1)
                dve.wait_ge(rstd_done, ln + 1)

            def normalise(j):
                nc.vector.tensor_scalar(x_in[:, j, :], x_in[:, j, :], mv[:, j, 0:1], rstd[:, j:j + 1],
                                        ALU.subtract, ALU.mult).then_inc(z_ready, 1)

            def lo_part(b, name, src, hi, lo):
                dve.wait_ge(hi_done, b * G + gid[name] + 1)
                nc.vector.tensor_tensor(lo, src, hi.bitcast(f32), ALU.subtract).then_inc(split_done, 1)

            def project(b, name):
                kind, blk, e = name
                hi, lo = (a[:, e, :] if kind == "q" else a[:, e, blk * NT:(blk + 1) * NT] for a in (qp if kind == "q" else kp))
                lo_part(b, name, staged[:, gid[name] % BANKS, :], hi, lo)

            def value(b, name):
                g, t = gid[name], name[1]
                dve.wait_ge(group_ready, b * G + g + 1)
                dve.wait_ge(split_done, free_at(b, name))
                nc.vector.tensor_tensor(staged[:, g % BANKS, :], bank[g % BANKS][:, :], bv[:, :], ALU.add) \
                    .then_inc(staged_dve, 1)
                dve.wait_ge(hi_done, b * G + g + 1)
                nc.vector.scalar_tensor_tensor(out=vp[1][:, t, :], in0=staged[:, g % BANKS, :], scalar=0.0,
                                               in1=vp[0][:, t, :].bitcast(f32), op0=ALU.max, op1=ALU.subtract) \
                    .then_inc(split_done, 1)

            def logits(b, name):
                g, u, k = gid[name], name[1], name[2]
                m = u * KT + k
                dve.wait_ge(group_ready, b * G + g + 1)
                dve.wait_ge(split_done, free_at(b, name))
                dve.wait_ge(mask_loaded[m % 2], 16 * (b * (UNITS * KT // 2) + m // 2 + 1))
                nc.vector.scalar_tensor_tensor(out=staged[:, g % BANKS, :], in0=bank[g % BANKS][:, :], scalar=0.0,
                                               in1=mask[:, m % 2, :], op0=ALU.max, op1=ALU.add).then_inc(staged_dve, 1)
                hi, lo = probs[k % PROBS]
                lo_part(b, name, staged[:, g % BANKS, :], hi, lo)

            def transposed(b, name):
                g, j = gid[name], name[2]
                cols = slice(j * P, (j + 1) * P)
                lo_part(b, name, bank[g % BANKS][:, :].rearrange("p (c n) -> p c n", c=DC), z_hi[:, :, cols], z_lo[:, :, cols])

            def residual(b, u):
                for j in range(TILES):
                    dve.wait_ge(relu_done, TILES * (b * UNITS + u) + j + 1)
                    dve.wait_ge(res_loaded[j], 16 * (b * UNITS + u + 1))
                    nc.vector.scalar_tensor_tensor(out=x_res[:, j, :], in0=acc[j][:, :], scalar=tg[:, 0:1],
                                                   in1=x_res[:, j, :], op0=ALU.mult, op1=ALU.add).then_inc(x2_ready, 1)

            for n in range(4):
                w_lo(n)
            ctx_part(0, 0, 0)
            ctx_part(0, 0, 1)
            for n in range(4, 8):
                w_lo(n)
            ctx_part(0, 0, 2)
            ctx_part(0, 0, 3)
            for n in range(8, W_PIECES):
                w_lo(n)

            def batch(b, last):
                for e in range(DC):
                    statistics(b * UNITS, e)
                    project(b, ("k", 0, e))
                value(b, ("v", 0))
                inverse(b * UNITS)
                for j in range(TILES):
                    normalise(j)
                value(b, ("v", 1))
                for j in range(TILES):
                    transposed(b, ("t", 0, j))
                for t in (2, 3):
                    value(b, ("v", t))
                for e in range(DC):
                    ctx_part(b, 1, e)
                    project(b, ("q", 0, e))
                for e in range(DC):
                    project(b, ("k", 1, e))
                for t in range(4, 8):
                    value(b, ("v", t))
                for k in range(5):
                    logits(b, ("s", 0, k))
                    if k < 2:
                        statistics(b * UNITS + 1, 2 * k)
                        statistics(b * UNITS + 1, 2 * k + 1)
                    if k == 2:
                        inverse(b * UNITS + 1)
                    if k in (2, 3):
                        normalise(2 * k - 4)
                        normalise(2 * k - 3)
                for j in range(TILES):
                    transposed(b, ("t", 1, j))
                for k in range(5, KT):
                    logits(b, ("s", 0, k))
                for e in range(DC):
                    project(b, ("q", 1, e))
                residual(b, 0)
                for k in range(KT):
                    logits(b, ("s", 1, k))
                    if last:
                        if k < 2:
                            statistics(LN_A, 2 * k)
                            statistics(LN_A, 2 * k + 1)
                        if k == 3:
                            inverse(LN_A)
                            for j in range(TILES):
                                normalise(j)
                    elif k < DC:
                        ctx_part(b + 1, 0, k)
                if last:
                    z2_parts(0)
                residual(b, 1)

            def z2_parts(t):
                for j in range(TILES):
                    cols = slice(j * P, (j + 1) * P)
                    dve.wait_ge(z2_hi_done, TILES * t + j + 1)
                    nc.vector.tensor_tensor(z2_lo[:, :, cols], bank[j][:, :].rearrange("p (c n) -> p c n", c=DC),
                                            z2_hi[:, :, cols].bitcast(f32), ALU.subtract).then_inc(z2_split, 1)

            with dve.Fori(0, LAST) as b:
                batch(b, False)
            batch(LAST, True)

            def result(t, j):
                dve.wait_ge(down_ready, TILES * t + j + 1)
                dve.wait_ge(res_loaded[j], 16 * (BLOCKS + t + 1))
                nc.vector.scalar_tensor_tensor(out=x_res[:, j, :], in0=acc[j][:, :], scalar=tg_ffn[:, 0:1],
                                               in1=x_res[:, j, :], op0=ALU.mult, op1=ALU.add).then_inc(y_ready, 1)

            def ffn_block(t, last):
                base = TILES + t * (2 * HC + TILES)
                for c in range(HC):
                    dve.wait_ge(ffn_ready, base + 2 * c + 2)
                    dve.wait_ge(silu_done, t * HC + c + 1)
                    s = staged[:, c % BANKS, :]
                    nc.vector.tensor_tensor(s, bank[(2 * c + 1) % BANKS][:, :], s, ALU.mult).then_inc(hid_full, 1)
                    dve.wait_ge(hid_hi_done, t * HC + c + 1)
                    nc.vector.tensor_tensor(hid[1][:, c, :], s, hid[0][:, c, :].bitcast(f32), ALU.subtract) \
                        .then_inc(hid_split, 1)
                    if not last and c in (4, 5, 6, 7):
                        statistics(LN_A + 1 + t, c - 4)
                if not last:
                    inverse(LN_A + 1 + t)
                    for j in range(TILES):
                        normalise(j)
                result(t, 0)
                if not last:
                    z2_parts(t + 1)
                for j in range(1, TILES):
                    result(t, j)

            with dve.Fori(0, BLOCKS - 1) as t:
                ffn_block(t, False)
            ffn_block(BLOCKS - 1, True)

        @block.tensor
        def _(pe):
            mm = nc.tensor.matmul

            def three_pass(dst, pairs, first=True, final=True):
                n, out = 3 * len(pairs), None
                terms = [t for lh, ll, rh, rl in pairs for t in ((lh, rh), (lh, rl), (ll, rh))]
                for i, (left, right) in enumerate(terms):
                    out = mm(dst, left, right, start=(first and i == 0), stop=(final and i == n - 1))
                return out

            def keys(b, blk, e):
                name = ("k", blk, e)
                pe.wait_ge(split_done, free_at(b, name))
                cols = slice(e * P, (e + 1) * P)
                three_pass(bank[gid[name] % BANKS][:, :],
                           [(wk_hi[:, c, cols], wk_lo[:, c, cols], ctx_hi[:, c, :], ctx_lo[:, c, :]) for c in range(DC)]) \
                    .then_inc(group_ready, 1)

            def queries(b, u, e):
                name = ("q", u, e)
                pe.wait_ge(split_done, free_at(b, name))
                cols = slice(e * P, (e + 1) * P)
                three_pass(bank[gid[name] % BANKS][:, :],
                           [(wq_hi[:, c, cols], wq_lo[:, c, cols], z_hi[:, c, :], z_lo[:, c, :]) for c in range(DC)]) \
                    .then_inc(group_ready, 1)

            def values(b, t):
                name = ("v", t)
                pe.wait_ge(split_done, free_at(b, name))
                cols = slice(t % TILES * P, (t % TILES + 1) * P)
                three_pass(bank[gid[name] % BANKS][:, :],
                           [(ctx_hi[:, c, cols], ctx_lo[:, c, cols], wv_hi[:, c, :], wv_lo[:, c, :]) for c in range(DC)]) \
                    .then_inc(group_ready, 1)

            def transposes(b, u):
                for j in range(TILES):
                    name = ("t", u, j)
                    pe.wait_ge(split_done, free_at(b, name))
                    pe.wait_ge(z_ready, TILES * (b * UNITS + u) + j + 1)
                    for c in range(DC):
                        t = nc.tensor.transpose(bank[gid[name] % BANKS][:, c * P:(c + 1) * P],
                                                x_in[:, j, c * P:(c + 1) * P], ident[:, :])
                    t.then_inc(group_ready, 1)

            def scores(b, u, k):
                name = ("s", u, k)
                pe.wait_ge(split_done, free_at(b, name))
                if k == 0:
                    pe.wait_ge(split_done, split_at(b, ("k", 1, DC - 1) if u == 0 else ("q", 1, DC - 1)))
                cols = slice(k * P, (k + 1) * P)
                three_pass(bank[gid[name] % BANKS][:, :],
                           [(kp[0][:, c, cols], kp[1][:, c, cols], qp[0][:, c, :], qp[1][:, c, :]) for c in range(DC)]) \
                    .then_inc(group_ready, 1)

            def attend(b, u, k):
                pe.wait_ge(split_done, split_at(b, ("s", u, k)))
                lh, ll = probs[k % PROBS]
                for j in range(TILES):
                    if k == 0:
                        pe.wait_ge(x2_ready, TILES * (b * UNITS + u) + j + 1)
                    cols = slice(j * P, (j + 1) * P)
                    last = three_pass(acc[j][:, :], [(lh[:, cols], ll[:, cols], vp[0][:, k, :], vp[1][:, k, :])],
                                      first=(k == 0), final=(k == KT - 1))
                    if k == KT - 1:
                        last.then_inc(acc_ready, 1)

            def z2_transposes(t):
                for j in range(TILES):
                    pe.wait_ge(z_ready, TILES * (LN_A + t) + j + 1)
                    for c in range(DC):
                        i = nc.tensor.transpose(bank[j][:, c * P:(c + 1) * P], x_in[:, j, c * P:(c + 1) * P], ident[:, :])
                    i.then_inc(ffn_ready, 1)

            pe.wait_ge(ident_set, 2)
            pe.wait_ge(w_split, W_PIECES)

            def batch(b, last):
                pe.wait_ge(ctx_split, b * CTX_PIECES + DC)
                for e in range(DC):
                    keys(b, 0, e)
                values(b, 0)
                values(b, 1)
                transposes(b, 0)
                values(b, 2)
                values(b, 3)
                pe.wait_ge(split_done, split_at(b, ("t", 0, TILES - 1)))
                for e in range(DC):
                    queries(b, 0, e)
                pe.wait_ge(ctx_split, b * CTX_PIECES + 2 * DC)
                for e in range(DC):
                    keys(b, 1, e)
                for t in range(4, 8):
                    values(b, t)
                for k in range(KT):
                    scores(b, 0, k)
                    if k >= LAG:
                        attend(b, 0, k - LAG)
                    if k == 4:
                        transposes(b, 1)
                pe.wait_ge(split_done, split_at(b, ("t", 1, TILES - 1)))
                for e in range(DC):
                    queries(b, 1, e)
                for k in range(KT - LAG, KT):
                    attend(b, 0, k)
                for k in range(KT):
                    scores(b, 1, k)
                    if k >= LAG:
                        attend(b, 1, k - LAG)
                if last:
                    pe.wait_ge(split_done, split_at(b, ("s", 1, KT - 1)))
                    z2_transposes(0)
                for k in range(KT - LAG, KT):
                    attend(b, 1, k)

            with pe.Fori(0, LAST) as b:
                batch(b, False)
            batch(LAST, True)

            pe.wait_ge(ffn_cast, FFN_PIECES)

            def ffn_block(t, last):
                pe.wait_ge(z2_split, TILES * (t + 1))
                for c in range(HC):
                    cols = slice(c * P, (c + 1) * P)
                    if c >= 2:
                        pe.wait_ge(hid_split, t * HC + c - 1)
                    for n, w in enumerate((ffn_gate, ffn_up)):
                        for i in range(2 * DC):
                            last_mm = mm(bank[(2 * c + n) % BANKS][:, :], w[:, i // 2, cols],
                                         (z2_hi, z2_lo)[i % 2][:, i // 2, :], start=(i == 0), stop=(i == 2 * DC - 1))
                        last_mm.then_inc(ffn_ready, 1)
                for j in range(TILES):
                    cols = slice(j * P, (j + 1) * P)
                    if j == 1 and not last:
                        pe.wait_ge(hid_split, (t + 1) * HC)
                        z2_transposes(t + 1)
                    for c in range(HC):
                        if j == 0:
                            pe.wait_ge(hid_split, t * HC + c + 1)
                        for n in range(2):
                            last_mm = mm(acc[j][:, :], hid[n][:, c, cols], ffn_down[:, c, :],
                                         start=(c == 0 and n == 0), stop=(c == HC - 1 and n == 1))
                    last_mm.then_inc(down_ready, 1)

            pe.wait_ge(x2_ready, TILES * (BLOCKS + 1))
            with pe.Fori(0, BLOCKS - 1) as t:
                ffn_block(t, False)
            ffn_block(BLOCKS - 1, True)


def kernel(x, ctx_1024, mask_1xSxS2_ff0, g_xattn, g_ffn, L0_xattn_kernel_q, L0_xattn_kernel_k, L0_xattn_kernel_v,
           L0_xattn_bias_q, L0_xattn_bias_k, L0_xattn_bias_v, L0_ffn_w_gate, L0_ffn_w_up, L0_ffn_w_down):
    import concourse.bacc as bacc
    from concourse.bass_utils import run_bass_kernel_spmd

    D = x.shape[-1]

    def columns(v):
        return np.ascontiguousarray(np.asarray(v).reshape(-1, 128).T)

    arrays = {
        "x": np.ascontiguousarray(x),
        "ctx_t": np.ascontiguousarray(np.asarray(ctx_1024).transpose(0, 2, 1)),
        "mask_t": np.ascontiguousarray(np.asarray(mask_1xSxS2_ff0)[0].T),
        "g_xattn": np.ascontiguousarray(g_xattn),
        "g_ffn": np.ascontiguousarray(g_ffn),
        "w_q": np.ascontiguousarray(np.asarray(L0_xattn_kernel_q).reshape(D, D)),
        "w_k": np.ascontiguousarray(np.asarray(L0_xattn_kernel_k).reshape(D, D)),
        "w_v": np.ascontiguousarray(np.asarray(L0_xattn_kernel_v).reshape(D, D)),
        "b_q": columns(L0_xattn_bias_q),
        "b_k": columns(L0_xattn_bias_k),
        "b_v": np.ascontiguousarray(L0_xattn_bias_v),
        "wg_t": np.ascontiguousarray(np.asarray(L0_ffn_w_gate).T),
        "wu_t": np.ascontiguousarray(np.asarray(L0_ffn_w_up).T),
        "wd_t": np.ascontiguousarray(np.asarray(L0_ffn_w_down).T),
    }
    nc = bacc.Bacc("TRN2", target_bir_lowering=False, num_devices=1)
    args = {name: nc.dram_tensor(f"{name}_dram", a.shape, mybir.dt.from_np(a.dtype), kind="ExternalInput").ap()
            for name, a in arrays.items()}
    out = nc.dram_tensor("out_dram", x.shape, mybir.dt.float32, kind="ExternalOutput").ap()
    x2 = nc.dram_tensor("x2_dram", x.shape, mybir.dt.float32, kind="Internal").ap()
    build(nc, *args.values(), out, x2)
    result = run_bass_kernel_spmd(nc, [{f"{name}_dram": a for name, a in arrays.items()}], core_ids=[0])
    return result.results[0]["out_dram"]
```

```python
import numpy as np
from contextlib import ExitStack
import concourse.bass as bass
from concourse import mybir


def build(nc, x, ctx_t, mask_t, g_xattn, g_ffn, w_q, w_k, w_v, b_q, b_k, b_v, wg_t, wu_t, wd_t, out, x2):
    f32, f32r, i32 = mybir.dt.float32, mybir.dt.float32r, mybir.dt.int32
    ALU = mybir.AluOpType
    ACT = mybir.ActivationFunctionType

    B, S, D = x.shape
    H = wg_t.shape[1]
    P = 128
    NT = 512
    DC, HC = D // P, H // P
    KT = S // P
    UNITS = S // NT
    TILES = NT // P
    BLOCKS = B * UNITS
    SCORE_SCALE = float(D) ** -0.5
    DEQUANT = 1.0 / 127.0
    EPS = 1e-5
    BANKS = 4
    LAG = 2
    PROBS = LAG + 1
    assert UNITS == 2 and TILES == DC == BANKS == 4

    order = ([("k", 0, e) for e in range(DC)] + [("v", t) for t in (0, 1)] + [("t", 0, j) for j in range(TILES)]
             + [("v", t) for t in (2, 3)] + [("q", 0, e) for e in range(DC)] + [("k", 1, e) for e in range(DC)]
             + [("v", t) for t in range(4, 8)] + [("s", 0, k) for k in range(5)] + [("t", 1, j) for j in range(TILES)]
             + [("s", 0, k) for k in range(5, KT)] + [("q", 1, e) for e in range(DC)] + [("s", 1, k) for k in range(KT)])
    G = len(order)
    assert G % BANKS == 0
    gid = {name: n for n, name in enumerate(order)}
    by_act = [name for name in order if name[0] in "kq"]
    by_dve = [name for name in order if name[0] in "vs"]
    aid = {name: n for n, name in enumerate(by_act)}
    vid = {name: n for n, name in enumerate(by_dve)}
    NA, NV = len(by_act), len(by_dve)

    es = ExitStack()
    with es:
        def sb(name, shape, dt=f32):
            return es.enter_context(nc.sbuf_tensor(name, shape, dt))

        def sem(name):
            return es.enter_context(nc.semaphore(name))

        OPW = DC * D
        operands = sb("operands", [P, 10 * OPW], f32r)

        def operand(n):
            return operands[:, n * OPW:(n + 1) * OPW].rearrange("p (c n) -> p c n", c=DC)
        wk_hi, wk_lo, wv_hi, wv_lo, ctx_hi, ctx_lo, wq_hi, wq_lo, z_hi, z_lo = (operand(n) for n in range(10))
        ffn_gate = operands[:, 0:DC * H].rearrange("p (c n) -> p c n", c=DC)
        ffn_up = operands[:, DC * H:2 * DC * H].rearrange("p (c n) -> p c n", c=DC)
        ffn_down = operands[:, 2 * DC * H:2 * DC * H + HC * D].rearrange("p (c n) -> p c n", c=HC)
        assert 2 * DC * H == 6 * OPW

        AW = DC * NT
        acts = sb("acts", [P, (2 + 4 + 4) * AW + PROBS * 2 * NT], f32r)
        qp = [acts[:, n * AW:(n + 1) * AW].rearrange("p (c n) -> p c n", c=DC) for n in (0, 1)]
        kp = [acts[:, (2 + 2 * n) * AW:(4 + 2 * n) * AW].rearrange("p (c n) -> p c n", c=DC) for n in (0, 1)]
        vp = [acts[:, (6 + 2 * n) * AW:(8 + 2 * n) * AW].rearrange("p (c n) -> p c n", c=KT) for n in (0, 1)]
        pr0 = 10 * AW
        probs = [[acts[:, pr0 + (2 * s + n) * NT:pr0 + (2 * s + n + 1) * NT] for n in (0, 1)] for s in range(PROBS)]
        z2_hi, z2_lo = qp
        hid = [acts[:, 2 * AW + n * HC * NT:2 * AW + (n + 1) * HC * NT].rearrange("p (c n) -> p c n", c=HC)
               for n in (0, 1)]

        raw = sb("raw", [P, 2, NT])
        x_in = sb("x_in", [P, TILES, D])
        x_res = sb("x_res", [P, TILES, D])
        mask = sb("mask", [P, 2, NT])
        staged = sb("staged", [P, BANKS, NT])
        bv = sb("bv", [P, D])
        bqk = sb("bqk", [P, 2, DC])
        bqs = sb("bqs", [P, DC])
        ident = sb("ident", [P, P])
        eps = sb("eps", [P, 1])
        gates = sb("gates", [P, 2])
        tg = sb("tg", [P, 2])
        tg_ffn = sb("tg_ffn", [P, 1])
        bn = sb("bn", [P, TILES, 6])
        mv = sb("mv", [P, TILES, 2])
        std = sb("std", [P, TILES])
        rstd = sb("rstd", [P, TILES])

        bank = [es.enter_context(nc.psum_tensor(f"bank{n}", [P, NT], f32)) for n in range(BANKS)]
        acc = [es.enter_context(nc.psum_tensor(f"acc{n}", [P, D], f32)) for n in range(TILES)]

        carrier = sem("carrier")
        small_loaded = sem("small_loaded")
        w_loaded = [sem(f"w_loaded{n}") for n in range(3 * DC)]
        first_loaded = [sem(f"first_loaded{n}") for n in range(DC)]
        w_hi_done, w_split = sem("w_hi_done"), sem("w_split")
        ident_set = sem("ident_set")
        consts_set, consts_ready = sem("consts_set"), sem("consts_ready")
        raw_loaded = [sem(f"raw_loaded{n}") for n in (0, 1)]
        ctx_in_mask = [sem(f"ctx_in_mask{n}") for n in (0, 1)]
        ctx_hi_done, ctx_split = sem("ctx_hi_done"), sem("ctx_split")
        x_loaded = [sem(f"x_loaded{n}") for n in range(TILES)]
        res_loaded = [sem(f"res_loaded{n}") for n in range(TILES)]
        stored = [sem(f"stored{n}") for n in range(TILES)]
        mask_loaded = [sem(f"mask_loaded{n}") for n in (0, 1)]
        bn_done, mv_done, std_done, rstd_done, z_ready = (sem(n) for n in
                                                          ("bn_done", "mv_done", "std_done", "rstd_done", "z_ready"))
        group_ready = sem("group_ready")
        staged_act, staged_dve = sem("staged_act"), sem("staged_dve")
        hi_done = sem("hi_done")
        split_done = sem("split_done")
        acc_ready, relu_done = sem("acc_ready"), sem("relu_done")
        x2_ready = sem("x2_ready")
        ffn_cast = sem("ffn_cast")
        ffn_ready = sem("ffn_ready")
        z2_hi_done, z2_split = sem("z2_hi_done"), sem("z2_split")
        silu_done, hid_full, hid_hi_done, hid_split = (sem(n) for n in ("silu_done", "hid_full", "hid_hi_done", "hid_split"))
        down_ready, y_ready = sem("down_ready"), sem("y_ready")

        def split_at(b, name):
            return b * G + gid[name] + 1 + BANKS

        def free_at(b, name):
            return b * G + gid[name] + 1

        LAST = B - 1
        W_PIECES = 3 * DC
        FFN_PIECES = 3 * HC
        CTX_PIECES = UNITS * DC
        CTX_ALL = B * CTX_PIECES
        LN_A = B * UNITS

        def w_piece(n):
            w, c = (w_k, w_v, w_q)[n // DC], n % DC
            hi, lo = ((wk_hi, wk_lo), (wv_hi, wv_lo), (wq_hi, wq_lo))[n // DC]
            slot = (staged[:, c, :], x_res[:, c, :], first_slot(c))[n // DC]
            return w[c * P:(c + 1) * P, :], slot, hi[:, c, :], lo[:, c, :]

        def first_slot(c):
            return raw[:, c, :] if c < 2 else mask[:, c - 2, :]

        RAW_FILLS = DC // 2 + 1

        def ctx_slot(blk, c):
            return mask[:, c - 2, :] if blk == 1 and c >= 2 else raw[:, c % 2, :]

        def ctx_loaded(b, blk, c):
            if blk == 1 and c >= 2:
                return ctx_in_mask[c - 2], 16 * (b + 1)
            return raw_loaded[c % 2], 16 * (b * RAW_FILLS + (c // 2 if blk == 0 else DC // 2) + 1 - DC // 2)

        def ffn_piece(n):
            kind, m = divmod(n, HC)
            if kind < 2:
                c, h = divmod(m, H // NT)
                src = (wg_t, wu_t)[kind][c * P:(c + 1) * P, h * NT:(h + 1) * NT]
                return src, (ffn_gate, ffn_up)[kind][:, c, h * NT:(h + 1) * NT]
            return wd_t[m * P:(m + 1) * P, :], ffn_down[:, m, :]

        block = es.enter_context(nc.Block())

        @block.sync
        def _(sp):
            def sp_wait(semaphore, value):
                sp.wait_ge(semaphore, value)
                sp.sem_inc(carrier, 1)

            def load_w(n):
                src, slot, _, _ = w_piece(n)
                sp.dma_start(slot, src).then_inc(w_loaded[n], 16)

            def load_ctx(b, blk, c):
                if blk == 1 and c >= 2:
                    sp_wait(split_done, split_at(b, ("k", 0, 0)))
                elif blk == 1:
                    sp_wait(ctx_split, b * CTX_PIECES + c + 3)
                elif c < 2:
                    sp_wait(ctx_split, b * CTX_PIECES + c - 3)
                else:
                    sp_wait(ctx_split, b * CTX_PIECES + c - 1)
                sp.dma_start(ctx_slot(blk, c), ctx_t[b, c * P:(c + 1) * P, blk * NT:(blk + 1) * NT]) \
                    .then_inc(ctx_loaded(b, blk, c)[0], 16)

            def load_x(b, u, j):
                r = u * NT + j * P
                sp.dma_start(x_in[:, j, :], x[b, r:r + P, :]).then_inc(x_loaded[j], 16)

            def load_res(b, u, j):
                r = u * NT + j * P
                sp.dma_start(x_res[:, j, :], x[b, r:r + P, :]).then_inc(res_loaded[j], 16)

            def store_x2(b, u):
                for j in range(TILES):
                    r = u * NT + j * P
                    sp_wait(x2_ready, TILES * (b * UNITS + u + 1) + j + 1)
                    sp.dma_start(x2[b, r:r + P, :], x_res[:, j, :]).then_inc(stored[j], 16)

            def load_ffn(n):
                if n < 2:
                    sp.wait_ge(ctx_split, CTX_ALL - DC + 1 + n)
                else:
                    sp.wait_ge(ffn_cast, n - 1)
                sp.dma_start(raw[:, n % 2, :].bitcast(i32), ffn_piece(n)[0]).then_inc(raw_loaded[n % 2], 16)

            for c in range(DC):
                load_w(c)
                sp.dma_start(first_slot(c), ctx_t[0, c * P:(c + 1) * P, 0:NT]).then_inc(first_loaded[c], 16)
            for c in range(DC):
                load_w(DC + c)
            for j in range(TILES):
                load_x(0, 0, j)
            for c in range(DC):
                sp.wait_ge(ctx_split, c + 1)
                load_w(2 * DC + c)
            sp.wait_ge(w_split, W_PIECES)
            for j in range(TILES):
                load_res(0, 0, j)

            def batch(b, last):
                for c in range(DC):
                    load_ctx(b, 1, c)
                for j in range(TILES):
                    sp_wait(group_ready, b * G + gid["t", 0, j] + 1)
                    load_x(b, 1, j)
                if last:
                    for n in range(10):
                        load_ffn(n)
                for j in range(TILES):
                    sp_wait(group_ready, b * G + gid["t", 1, j] + 1)
                    if last:
                        sp.dma_start(x_in[:, j, :], x2[0, j * P:(j + 1) * P, :]).then_inc(x_loaded[j], 16)
                    else:
                        load_x(b + 1, 0, j)
                if last:
                    for n in range(10, 20):
                        load_ffn(n)
                else:
                    for c in range(2):
                        load_ctx(b + 1, 0, c)
                store_x2(b, 0)
                for j in range(TILES):
                    sp_wait(stored[j], 16 * (b * UNITS + 1))
                    load_res(b, 1, j)
                if last:
                    for n in range(20, FFN_PIECES):
                        load_ffn(n)
                else:
                    for c in range(2, DC):
                        load_ctx(b + 1, 0, c)
                store_x2(b, 1)
                if not last:
                    for j in range(TILES):
                        sp_wait(stored[j], 16 * (b * UNITS + 2))
                        load_res(b + 1, 0, j)

            with sp.Fori(0, LAST) as b:
                batch(b, False)
            batch(LAST, True)

            for j in range(TILES):
                sp.wait_ge(stored[j], 16 * BLOCKS)
            x2_rows = x2.rearrange("b (t n) d -> (b t) n d", n=NT)
            out_rows = out.rearrange("b (t n) d -> (b t) n d", n=NT)

            def ffn_block(t, last):
                if not last:
                    for j in range(TILES):
                        sp_wait(ffn_ready, t * (2 * HC + TILES) + j + 1)
                        sp.dma_start(x_in[:, j, :], x2_rows[t + 1, j * P:(j + 1) * P, :]).then_inc(x_loaded[j], 16)
                for j in range(TILES):
                    sp_wait(stored[j], 16 * (BLOCKS + t))
                    sp.dma_start(x_res[:, j, :], x2_rows[t, j * P:(j + 1) * P, :]).then_inc(res_loaded[j], 16)
                for j in range(TILES):
                    sp_wait(y_ready, TILES * t + j + 1)
                    sp.dma_start(out_rows[t, j * P:(j + 1) * P, :], x_res[:, j, :]).then_inc(stored[j], 16)

            with sp.Fori(0, BLOCKS - 1) as t:
                ffn_block(t, False)
            ffn_block(BLOCKS - 1, True)
            for j in range(TILES):
                sp.wait_ge(stored[j], 16 * 2 * BLOCKS)

        @block.gpsimd
        def _(pool):
            pool.dma_start(bqk[:, 0, :], b_q).then_inc(small_loaded, 16)
            pool.dma_start(bqk[:, 1, :], b_k).then_inc(small_loaded, 16)
            pool.dma_start(bv[:, :], b_v.rearrange("(a n) -> a n", a=1).to_broadcast([P, D])).then_inc(small_loaded, 16)
            pool.dma_start(gates[:, 0:1], g_xattn.rearrange("(a n) -> a n", a=1).to_broadcast([P, 1])) \
                .then_inc(small_loaded, 16)
            pool.dma_start(gates[:, 1:2], g_ffn.rearrange("(a n) -> a n", a=1).to_broadcast([P, 1])) \
                .then_inc(small_loaded, 16)
            pool.memset(ident[:, :], 0.0).then_inc(ident_set, 1)
            pool.wait_ge(ident_set, 1)
            pool.affine_select(out=ident[:, :], in_=ident[:, :], compare_op=ALU.not_equal, fill=1.0, base=0,
                               pattern=[[-1, P]], channel_multiplier=1).then_inc(ident_set, 1)
            with pool.Fori(0, B) as b:
                for m in range(UNITS * KT):
                    u, k = divmod(m, KT)
                    if m < 2:
                        pool.wait_ge(ctx_split, (b + 1) * CTX_PIECES)
                    else:
                        pool.wait_ge(staged_dve, b * NV + vid["s", (m - 2) // KT, (m - 2) % KT] + 1)
                    pool.sem_inc(carrier, 1)
                    pool.dma_start(mask[:, m % 2, :], mask_t[k * P:(k + 1) * P, u * NT:(u + 1) * NT]) \
                        .then_inc(mask_loaded[m % 2], 16)

        @block.scalar
        def _(act):
            act.wait_ge(small_loaded, 16 * 5)
            nc.scalar.activation(tg[:, :], gates[:, :], ACT.Tanh).then_inc(consts_ready, 1)
            nc.scalar.activation(bqs[:, :], bqk[:, 0, :], ACT.Copy, scale=SCORE_SCALE).then_inc(consts_ready, 1)
            act.wait_ge(consts_ready, 2)

            def w_hi(n):
                _, slot, hi, _ = w_piece(n)
                act.wait_ge(w_loaded[n], 16)
                nc.scalar.activation(hi, slot, ACT.Copy).then_inc(w_hi_done, 1)

            def ctx_part(b, blk, c):
                act.wait_ge(*ctx_loaded(b, blk, c))
                nc.scalar.activation(ctx_hi[:, c, :], ctx_slot(blk, c), ACT.Copy).then_inc(ctx_hi_done, 1)

            def ffn_weights(n):
                act.wait_ge(raw_loaded[n % 2], 16 * (B * RAW_FILLS - DC // 2 + n // 2 + 1))
                nc.scalar.activation(ffn_piece(n)[1], raw[:, n % 2, :].bitcast(i32), ACT.Copy).then_inc(ffn_cast, 1)

            def project(b, name):
                g = gid[name]
                kind, blk, e = name
                act.wait_ge(group_ready, b * G + g + 1)
                act.wait_ge(split_done, free_at(b, name))
                bias, scale = (bqs[:, e:e + 1], SCORE_SCALE) if kind == "q" else (bqk[:, 1, e:e + 1], 1.0)
                nc.scalar.activation(staged[:, g % BANKS, :], bank[g % BANKS][:, :], ACT.Relu, bias=bias,
                                     scale=scale).then_inc(staged_act, 1)
                act.wait_ge(staged_act, b * NA + aid[name] + 1)
                dst = qp[0][:, e, :] if kind == "q" else kp[0][:, e, blk * NT:(blk + 1) * NT]
                nc.scalar.activation(dst, staged[:, g % BANKS, :], ACT.Copy).then_inc(hi_done, 1)

            def value(b, name):
                g = gid[name]
                act.wait_ge(staged_dve, b * NV + vid[name] + 1)
                nc.scalar.activation(vp[0][:, name[1], :], staged[:, g % BANKS, :], ACT.Relu).then_inc(hi_done, 1)

            def logits(b, name):
                g = gid[name]
                act.wait_ge(staged_dve, b * NV + vid[name] + 1)
                nc.scalar.activation(probs[name[2] % PROBS][0], staged[:, g % BANKS, :], ACT.Copy).then_inc(hi_done, 1)

            def transposed(b, name):
                g = gid[name]
                act.wait_ge(group_ready, b * G + g + 1)
                nc.scalar.activation(z_hi[:, :, name[2] * P:(name[2] + 1) * P],
                                     bank[g % BANKS][:, :].rearrange("p (c n) -> p c n", c=DC), ACT.Copy) \
                    .then_inc(hi_done, 1)

            def square_root(ln):
                act.wait_ge(mv_done, TILES * (ln + 1))
                nc.scalar.activation(std[:, :], mv[:, :, 1], ACT.Sqrt, bias=eps[:, 0:1]).then_inc(std_done, 1)

            def attended(b, u):
                for j in range(TILES):
                    act.wait_ge(acc_ready, TILES * (b * UNITS + u) + j + 1)
                    nc.scalar.activation(acc[j][:, :], acc[j][:, :], ACT.Relu).then_inc(relu_done, 1)

            for c in range(DC):
                w_hi(c)
                act.wait_ge(first_loaded[c], 16)
                nc.scalar.activation(ctx_hi[:, c, :], first_slot(c), ACT.Copy).then_inc(ctx_hi_done, 1)
            for n in range(DC, W_PIECES):
                w_hi(n)
            act.wait_ge(consts_set, 1)
            act.wait_ge(w_split, W_PIECES)

            def batch(b, last):
                for e in range(DC):
                    project(b, ("k", 0, e))
                    if e == 1:
                        square_root(b * UNITS)
                for t in (0, 1):
                    value(b, ("v", t))
                for j in range(TILES):
                    transposed(b, ("t", 0, j))
                for t in (2, 3):
                    value(b, ("v", t))
                for e in range(DC):
                    ctx_part(b, 1, e)
                    project(b, ("q", 0, e))
                for e in range(DC):
                    project(b, ("k", 1, e))
                for t in range(4, 8):
                    value(b, ("v", t))
                for k in range(5):
                    logits(b, ("s", 0, k))
                    if k == 1:
                        square_root(b * UNITS + 1)
                    if last:
                        ffn_weights(2 * k)
                        ffn_weights(2 * k + 1)
                for j in range(TILES):
                    transposed(b, ("t", 1, j))
                for k in range(5, KT):
                    logits(b, ("s", 0, k))
                    if last:
                        ffn_weights(2 * k)
                        ffn_weights(2 * k + 1)
                for e in range(DC):
                    project(b, ("q", 1, e))
                    if last:
                        ffn_weights(2 * KT + e)
                attended(b, 0)
                for k in range(KT):
                    logits(b, ("s", 1, k))
                    if last:
                        ffn_weights(2 * KT + DC + 2 * k)
                        ffn_weights(2 * KT + DC + 2 * k + 1)
                    if last and k == 2:
                        square_root(LN_A)
                    if not last and k < DC:
                        ctx_part(b + 1, 0, k)
                if last:
                    z2_parts(0)
                attended(b, 1)

            def z2_parts(t):
                for j in range(TILES):
                    act.wait_ge(ffn_ready, t * (2 * HC + TILES) + j + 1)
                    nc.scalar.activation(z2_hi[:, :, j * P:(j + 1) * P],
                                         bank[j][:, :].rearrange("p (c n) -> p c n", c=DC), ACT.Copy) \
                        .then_inc(z2_hi_done, 1)

            with act.Fori(0, LAST) as b:
                batch(b, False)
            batch(LAST, True)

            def ffn_block(t, last):
                base = TILES + t * (2 * HC + TILES)
                for c in range(HC):
                    act.wait_ge(ffn_ready, base + 2 * c + 1)
                    if c >= BANKS:
                        act.wait_ge(hid_split, t * HC + c - BANKS + 1)
                    nc.scalar.activation(staged[:, c % BANKS, :], bank[2 * c % BANKS][:, :], ACT.Silu, scale=DEQUANT) \
                        .then_inc(silu_done, 1)
                    act.wait_ge(hid_full, t * HC + c + 1)
                    nc.scalar.activation(hid[0][:, c, :], staged[:, c % BANKS, :], ACT.Copy).then_inc(hid_hi_done, 1)
                if not last:
                    square_root(LN_A + 1 + t)
                    z2_parts(t + 1)

            with act.Fori(0, BLOCKS - 1) as t:
                ffn_block(t, False)
            ffn_block(BLOCKS - 1, True)

        @block.vector
        def _(dve):
            nc.vector.memset(eps[:, :], EPS).then_inc(consts_set, 1)
            dve.sem_inc(split_done, BANKS)
            dve.sem_inc(x2_ready, TILES)
            dve.wait_ge(consts_ready, 2)
            nc.vector.tensor_scalar(tg_ffn[:, :], tg[:, 1:2], DEQUANT, DEQUANT, ALU.mult, ALU.mult).then_inc(consts_set, 1)

            def w_lo(n):
                _, slot, hi, lo = w_piece(n)
                dve.wait_ge(w_hi_done, n + 1)
                nc.vector.tensor_tensor(lo, slot, hi.bitcast(f32), ALU.subtract).then_inc(w_split, 1)

            def ctx_part(b, blk, c):
                n = blk * DC + c
                dve.wait_ge(ctx_hi_done, b * CTX_PIECES + n + 1)
                nc.vector.tensor_tensor(ctx_lo[:, c, :], ctx_slot(blk, c), ctx_hi[:, c, :].bitcast(f32), ALU.subtract) \
                    .then_inc(ctx_split, 1)

            def statistics(ln, j):
                dve.wait_ge(x_loaded[j], 16 * (ln + 1))
                nc.vector.bn_stats(bn[:, j, :], x_in[:, j, :]).then_inc(bn_done, 1)
                dve.wait_ge(bn_done, TILES * ln + j + 1)
                dve.sem_inc(carrier, 1)
                nc.vector.bn_aggr(mv[:, j, :], bn[:, j, :]).then_inc(mv_done, 1)

            def inverse(ln):
                dve.wait_ge(std_done, ln + 1)
                nc.vector.reciprocal(rstd[:, :], std[:, :]).then_inc(rstd_done, 1)
                dve.wait_ge(rstd_done, ln + 1)

            def normalise(j):
                nc.vector.tensor_scalar(x_in[:, j, :], x_in[:, j, :], mv[:, j, 0:1], rstd[:, j:j + 1],
                                        ALU.subtract, ALU.mult).then_inc(z_ready, 1)

            def lo_part(b, name, src, hi, lo):
                dve.wait_ge(hi_done, b * G + gid[name] + 1)
                nc.vector.tensor_tensor(lo, src, hi.bitcast(f32), ALU.subtract).then_inc(split_done, 1)

            def project(b, name):
                kind, blk, e = name
                hi, lo = (a[:, e, :] if kind == "q" else a[:, e, blk * NT:(blk + 1) * NT] for a in (qp if kind == "q" else kp))
                lo_part(b, name, staged[:, gid[name] % BANKS, :], hi, lo)

            def value(b, name):
                g, t = gid[name], name[1]
                dve.wait_ge(group_ready, b * G + g + 1)
                dve.wait_ge(split_done, free_at(b, name))
                nc.vector.tensor_tensor(staged[:, g % BANKS, :], bank[g % BANKS][:, :], bv[:, :], ALU.add) \
                    .then_inc(staged_dve, 1)
                dve.wait_ge(hi_done, b * G + g + 1)
                nc.vector.scalar_tensor_tensor(out=vp[1][:, t, :], in0=staged[:, g % BANKS, :], scalar=0.0,
                                               in1=vp[0][:, t, :].bitcast(f32), op0=ALU.max, op1=ALU.subtract) \
                    .then_inc(split_done, 1)

            def logits(b, name):
                g, u, k = gid[name], name[1], name[2]
                m = u * KT + k
                dve.wait_ge(group_ready, b * G + g + 1)
                dve.wait_ge(split_done, free_at(b, name))
                dve.wait_ge(mask_loaded[m % 2], 16 * (b * (UNITS * KT // 2) + m // 2 + 1))
                nc.vector.scalar_tensor_tensor(out=staged[:, g % BANKS, :], in0=bank[g % BANKS][:, :], scalar=0.0,
                                               in1=mask[:, m % 2, :], op0=ALU.max, op1=ALU.add).then_inc(staged_dve, 1)
                hi, lo = probs[k % PROBS]
                lo_part(b, name, staged[:, g % BANKS, :], hi, lo)

            def transposed(b, name):
                g, j = gid[name], name[2]
                cols = slice(j * P, (j + 1) * P)
                lo_part(b, name, bank[g % BANKS][:, :].rearrange("p (c n) -> p c n", c=DC), z_hi[:, :, cols], z_lo[:, :, cols])

            def residual(b, u):
                for j in range(TILES):
                    dve.wait_ge(relu_done, TILES * (b * UNITS + u) + j + 1)
                    dve.wait_ge(res_loaded[j], 16 * (b * UNITS + u + 1))
                    nc.vector.scalar_tensor_tensor(out=x_res[:, j, :], in0=acc[j][:, :], scalar=tg[:, 0:1],
                                                   in1=x_res[:, j, :], op0=ALU.mult, op1=ALU.add).then_inc(x2_ready, 1)

            for c in range(DC):
                w_lo(c)
                dve.wait_ge(ctx_hi_done, c + 1)
                nc.vector.tensor_tensor(ctx_lo[:, c, :], first_slot(c), ctx_hi[:, c, :].bitcast(f32), ALU.subtract) \
                    .then_inc(ctx_split, 1)
            for n in range(DC, W_PIECES):
                w_lo(n)

            def batch(b, last):
                for e in range(DC):
                    if e < 2:
                        statistics(b * UNITS, 2 * e)
                        statistics(b * UNITS, 2 * e + 1)
                    project(b, ("k", 0, e))
                    if e == 2:
                        inverse(b * UNITS)
                    if e >= 2:
                        normalise(2 * e - 4)
                        normalise(2 * e - 3)
                for t in (0, 1):
                    value(b, ("v", t))
                for j in range(TILES):
                    transposed(b, ("t", 0, j))
                for t in (2, 3):
                    value(b, ("v", t))
                for e in range(DC):
                    ctx_part(b, 1, e)
                    project(b, ("q", 0, e))
                for e in range(DC):
                    project(b, ("k", 1, e))
                for t in range(4, 8):
                    value(b, ("v", t))
                for k in range(5):
                    logits(b, ("s", 0, k))
                    if k < 2:
                        statistics(b * UNITS + 1, 2 * k)
                        statistics(b * UNITS + 1, 2 * k + 1)
                    if k == 2:
                        inverse(b * UNITS + 1)
                    if k in (2, 3):
                        normalise(2 * k - 4)
                        normalise(2 * k - 3)
                for j in range(TILES):
                    transposed(b, ("t", 1, j))
                for k in range(5, KT):
                    logits(b, ("s", 0, k))
                for e in range(DC):
                    project(b, ("q", 1, e))
                residual(b, 0)
                for k in range(KT):
                    logits(b, ("s", 1, k))
                    if last:
                        if k < 2:
                            statistics(LN_A, 2 * k)
                            statistics(LN_A, 2 * k + 1)
                        if k == 3:
                            inverse(LN_A)
                            for j in range(TILES):
                                normalise(j)
                    elif k < DC:
                        ctx_part(b + 1, 0, k)
                if last:
                    z2_parts(0)
                residual(b, 1)

            def z2_parts(t):
                for j in range(TILES):
                    cols = slice(j * P, (j + 1) * P)
                    dve.wait_ge(z2_hi_done, TILES * t + j + 1)
                    nc.vector.tensor_tensor(z2_lo[:, :, cols], bank[j][:, :].rearrange("p (c n) -> p c n", c=DC),
                                            z2_hi[:, :, cols].bitcast(f32), ALU.subtract).then_inc(z2_split, 1)

            with dve.Fori(0, LAST) as b:
                batch(b, False)
            batch(LAST, True)

            def result(t, j):
                dve.wait_ge(down_ready, TILES * t + j + 1)
                dve.wait_ge(res_loaded[j], 16 * (BLOCKS + t + 1))
                nc.vector.scalar_tensor_tensor(out=x_res[:, j, :], in0=acc[j][:, :], scalar=tg_ffn[:, 0:1],
                                               in1=x_res[:, j, :], op0=ALU.mult, op1=ALU.add).then_inc(y_ready, 1)

            def ffn_block(t, last):
                base = TILES + t * (2 * HC + TILES)
                for c in range(HC):
                    dve.wait_ge(ffn_ready, base + 2 * c + 2)
                    dve.wait_ge(silu_done, t * HC + c + 1)
                    s = staged[:, c % BANKS, :]
                    nc.vector.tensor_tensor(s, bank[(2 * c + 1) % BANKS][:, :], s, ALU.mult).then_inc(hid_full, 1)
                    dve.wait_ge(hid_hi_done, t * HC + c + 1)
                    nc.vector.tensor_tensor(hid[1][:, c, :], s, hid[0][:, c, :].bitcast(f32), ALU.subtract) \
                        .then_inc(hid_split, 1)
                    if not last and c in (4, 5, 6, 7):
                        statistics(LN_A + 1 + t, c - 4)
                if not last:
                    inverse(LN_A + 1 + t)
                    for j in range(TILES):
                        normalise(j)
                result(t, 0)
                if not last:
                    z2_parts(t + 1)
                for j in range(1, TILES):
                    result(t, j)

            with dve.Fori(0, BLOCKS - 1) as t:
                ffn_block(t, False)
            ffn_block(BLOCKS - 1, True)

        @block.tensor
        def _(pe):
            mm = nc.tensor.matmul

            def three_pass(dst, pairs, first=True, final=True):
                n, out = 3 * len(pairs), None
                terms = [t for lh, ll, rh, rl in pairs for t in ((lh, rh), (lh, rl), (ll, rh))]
                for i, (left, right) in enumerate(terms):
                    out = mm(dst, left, right, start=(first and i == 0), stop=(final and i == n - 1))
                return out

            def keys(b, blk, e):
                name = ("k", blk, e)
                pe.wait_ge(split_done, free_at(b, name))
                cols = slice(e * P, (e + 1) * P)
                three_pass(bank[gid[name] % BANKS][:, :],
                           [(wk_hi[:, c, cols], wk_lo[:, c, cols], ctx_hi[:, c, :], ctx_lo[:, c, :]) for c in range(DC)]) \
                    .then_inc(group_ready, 1)

            def queries(b, u, e):
                name = ("q", u, e)
                pe.wait_ge(split_done, free_at(b, name))
                cols = slice(e * P, (e + 1) * P)
                three_pass(bank[gid[name] % BANKS][:, :],
                           [(wq_hi[:, c, cols], wq_lo[:, c, cols], z_hi[:, c, :], z_lo[:, c, :]) for c in range(DC)]) \
                    .then_inc(group_ready, 1)

            def values(b, t):
                name = ("v", t)
                pe.wait_ge(split_done, free_at(b, name))
                cols = slice(t % TILES * P, (t % TILES + 1) * P)
                three_pass(bank[gid[name] % BANKS][:, :],
                           [(ctx_hi[:, c, cols], ctx_lo[:, c, cols], wv_hi[:, c, :], wv_lo[:, c, :]) for c in range(DC)]) \
                    .then_inc(group_ready, 1)

            def transposes(b, u):
                for j in range(TILES):
                    name = ("t", u, j)
                    pe.wait_ge(split_done, free_at(b, name))
                    pe.wait_ge(z_ready, TILES * (b * UNITS + u) + j + 1)
                    for c in range(DC):
                        t = nc.tensor.transpose(bank[gid[name] % BANKS][:, c * P:(c + 1) * P],
                                                x_in[:, j, c * P:(c + 1) * P], ident[:, :])
                    t.then_inc(group_ready, 1)

            def scores(b, u, k):
                name = ("s", u, k)
                pe.wait_ge(split_done, free_at(b, name))
                if k == 0:
                    pe.wait_ge(split_done, split_at(b, ("k", 1, DC - 1) if u == 0 else ("q", 1, DC - 1)))
                cols = slice(k * P, (k + 1) * P)
                three_pass(bank[gid[name] % BANKS][:, :],
                           [(kp[0][:, c, cols], kp[1][:, c, cols], qp[0][:, c, :], qp[1][:, c, :]) for c in range(DC)]) \
                    .then_inc(group_ready, 1)

            def attend(b, u, k):
                pe.wait_ge(split_done, split_at(b, ("s", u, k)))
                lh, ll = probs[k % PROBS]
                for j in range(TILES):
                    if k == 0:
                        pe.wait_ge(x2_ready, TILES * (b * UNITS + u) + j + 1)
                    cols = slice(j * P, (j + 1) * P)
                    last = three_pass(acc[j][:, :], [(lh[:, cols], ll[:, cols], vp[0][:, k, :], vp[1][:, k, :])],
                                      first=(k == 0), final=(k == KT - 1))
                    if k == KT - 1:
                        last.then_inc(acc_ready, 1)

            def z2_transposes(t):
                for j in range(TILES):
                    pe.wait_ge(z_ready, TILES * (LN_A + t) + j + 1)
                    for c in range(DC):
                        i = nc.tensor.transpose(bank[j][:, c * P:(c + 1) * P], x_in[:, j, c * P:(c + 1) * P], ident[:, :])
                    i.then_inc(ffn_ready, 1)

            pe.wait_ge(ident_set, 2)

            def batch(b, last):
                pe.wait_ge(w_split, DC)
                pe.wait_ge(ctx_split, b * CTX_PIECES + DC)
                for e in range(DC):
                    keys(b, 0, e)
                pe.wait_ge(w_split, 2 * DC)
                values(b, 0)
                values(b, 1)
                transposes(b, 0)
                values(b, 2)
                values(b, 3)
                pe.wait_ge(w_split, 3 * DC)
                pe.wait_ge(split_done, split_at(b, ("t", 0, TILES - 1)))
                for e in range(DC):
                    queries(b, 0, e)
                pe.wait_ge(ctx_split, b * CTX_PIECES + 2 * DC)
                for e in range(DC):
                    keys(b, 1, e)
                for t in range(4, 8):
                    values(b, t)
                for k in range(KT):
                    scores(b, 0, k)
                    if k >= LAG:
                        attend(b, 0, k - LAG)
                    if k == 4:
                        transposes(b, 1)
                pe.wait_ge(split_done, split_at(b, ("t", 1, TILES - 1)))
                for e in range(DC):
                    queries(b, 1, e)
                for k in range(KT - LAG, KT):
                    attend(b, 0, k)
                for k in range(KT):
                    scores(b, 1, k)
                    if k >= LAG:
                        attend(b, 1, k - LAG)
                if last:
                    pe.wait_ge(split_done, split_at(b, ("s", 1, KT - 1)))
                    z2_transposes(0)
                for k in range(KT - LAG, KT):
                    attend(b, 1, k)

            with pe.Fori(0, LAST) as b:
                batch(b, False)
            batch(LAST, True)

            pe.wait_ge(ffn_cast, FFN_PIECES)

            def ffn_block(t, last):
                pe.wait_ge(z2_split, TILES * (t + 1))
                for c in range(HC):
                    cols = slice(c * P, (c + 1) * P)
                    if c >= 2:
                        pe.wait_ge(hid_split, t * HC + c - 1)
                    for n, w in enumerate((ffn_gate, ffn_up)):
                        for i in range(2 * DC):
                            last_mm = mm(bank[(2 * c + n) % BANKS][:, :], w[:, i // 2, cols],
                                         (z2_hi, z2_lo)[i % 2][:, i // 2, :], start=(i == 0), stop=(i == 2 * DC - 1))
                        last_mm.then_inc(ffn_ready, 1)
                for j in range(TILES):
                    cols = slice(j * P, (j + 1) * P)
                    if j == 1 and not last:
                        pe.wait_ge(hid_split, (t + 1) * HC)
                        z2_transposes(t + 1)
                    for c in range(HC):
                        if j == 0:
                            pe.wait_ge(hid_split, t * HC + c + 1)
                        for n in range(2):
                            last_mm = mm(acc[j][:, :], hid[n][:, c, cols], ffn_down[:, c, :],
                                         start=(c == 0 and n == 0), stop=(c == HC - 1 and n == 1))
                    last_mm.then_inc(down_ready, 1)

            pe.wait_ge(x2_ready, TILES * (BLOCKS + 1))
            with pe.Fori(0, BLOCKS - 1) as t:
                ffn_block(t, False)
            ffn_block(BLOCKS - 1, True)


def kernel(x, ctx_1024, mask_1xSxS2_ff0, g_xattn, g_ffn, L0_xattn_kernel_q, L0_xattn_kernel_k, L0_xattn_kernel_v,
           L0_xattn_bias_q, L0_xattn_bias_k, L0_xattn_bias_v, L0_ffn_w_gate, L0_ffn_w_up, L0_ffn_w_down):
    import concourse.bacc as bacc
    from concourse.bass_utils import run_bass_kernel_spmd

    D = x.shape[-1]

    def columns(v):
        return np.ascontiguousarray(np.asarray(v).reshape(-1, 128).T)

    arrays = {
        "x": np.ascontiguousarray(x),
        "ctx_t": np.ascontiguousarray(np.asarray(ctx_1024).transpose(0, 2, 1)),
        "mask_t": np.ascontiguousarray(np.asarray(mask_1xSxS2_ff0)[0].T),
        "g_xattn": np.ascontiguousarray(g_xattn),
        "g_ffn": np.ascontiguousarray(g_ffn),
        "w_q": np.ascontiguousarray(np.asarray(L0_xattn_kernel_q).reshape(D, D)),
        "w_k": np.ascontiguousarray(np.asarray(L0_xattn_kernel_k).reshape(D, D)),
        "w_v": np.ascontiguousarray(np.asarray(L0_xattn_kernel_v).reshape(D, D)),
        "b_q": columns(L0_xattn_bias_q),
        "b_k": columns(L0_xattn_bias_k),
        "b_v": np.ascontiguousarray(L0_xattn_bias_v),
        "wg_t": np.ascontiguousarray(np.asarray(L0_ffn_w_gate).T),
        "wu_t": np.ascontiguousarray(np.asarray(L0_ffn_w_up).T),
        "wd_t": np.ascontiguousarray(np.asarray(L0_ffn_w_down).T),
    }
    nc = bacc.Bacc("TRN2", target_bir_lowering=False, num_devices=1)
    args = {name: nc.dram_tensor(f"{name}_dram", a.shape, mybir.dt.from_np(a.dtype), kind="ExternalInput").ap()
            for name, a in arrays.items()}
    out = nc.dram_tensor("out_dram", x.shape, mybir.dt.float32, kind="ExternalOutput").ap()
    x2 = nc.dram_tensor("x2_dram", x.shape, mybir.dt.float32, kind="Internal").ap()
    build(nc, *args.values(), out, x2)
    result = run_bass_kernel_spmd(nc, [{f"{name}_dram": a for name, a in arrays.items()}], core_ids=[0])
    return result.results[0]["out_dram"]
```

```python
import numpy as np
from contextlib import ExitStack
import concourse.bass as bass
from concourse import mybir


def build(nc, x, ctx_t, mask_t, g_xattn, g_ffn, w_q, w_k, w_v, b_q, b_k, b_v, wg_t, wu_t, wd_t, out, x2):
    f32, f32r, i32 = mybir.dt.float32, mybir.dt.float32r, mybir.dt.int32
    ALU = mybir.AluOpType
    ACT = mybir.ActivationFunctionType
    AX = mybir.AxisListType
    RMAX = bass.bass_isa.ReduceOp.max

    B, S, D = x.shape
    H = wg_t.shape[1]
    P = 128
    NT = 512
    DC, HC = D // P, H // P
    KT = S // P
    UNITS = S // NT
    TILES = NT // P
    BLOCKS = B * UNITS
    SCORE_SCALE = float(D) ** -0.5
    DEQUANT = 1.0 / 127.0
    EPS = 1e-5
    BANKS = 4
    LAG = 2
    PROBS = LAG + 1
    assert UNITS == 2 and TILES == DC == BANKS == 4

    SQ = 32
    QUADS = P // SQ
    SLABS = NT // SQ
    SLABS_T = SLABS // TILES
    assert QUADS * P == D and QUADS == DC

    order = ([("k", 0, e) for e in range(DC)] + [("v", t) for t in range(4)] + [("q", 0, e) for e in range(DC)]
             + [("k", 1, e) for e in range(DC)] + [("v", t) for t in range(4, 8)]
             + [("s", 0, k) for k in range(KT)] + [("q", 1, e) for e in range(DC)] + [("s", 1, k) for k in range(KT)])
    G = len(order)
    assert G % BANKS == 0
    gid = {name: n for n, name in enumerate(order)}
    by_act = [name for name in order if name[0] in "kq"]
    by_dve = [name for name in order if name[0] in "vs"]
    aid = {name: n for n, name in enumerate(by_act)}
    vid = {name: n for n, name in enumerate(by_dve)}
    NA, NV = len(by_act), len(by_dve)

    es = ExitStack()
    with es:
        def sb(name, shape, dt=f32):
            return es.enter_context(nc.sbuf_tensor(name, shape, dt))

        def sem(name):
            return es.enter_context(nc.semaphore(name))

        OPW = DC * D
        operands = sb("operands", [P, 10 * OPW], f32r)

        def operand(n):
            return operands[:, n * OPW:(n + 1) * OPW].rearrange("p (c n) -> p c n", c=DC)
        wk_hi, wk_lo, wv_hi, wv_lo, ctx_hi, ctx_lo, wq_hi, wq_lo, z_hi, z_lo = (operand(n) for n in range(10))
        ffn_gate = operands[:, 0:DC * H].rearrange("p (c n) -> p c n", c=DC)
        ffn_up = operands[:, DC * H:2 * DC * H].rearrange("p (c n) -> p c n", c=DC)
        ffn_down = operands[:, 2 * DC * H:2 * DC * H + HC * D].rearrange("p (c n) -> p c n", c=HC)
        assert 2 * DC * H == 6 * OPW

        AW = DC * NT
        acts = sb("acts", [P, (2 + 4 + 4) * AW + PROBS * 2 * NT], f32r)
        qp = [acts[:, n * AW:(n + 1) * AW].rearrange("p (c n) -> p c n", c=DC) for n in (0, 1)]
        kp = [acts[:, (2 + 2 * n) * AW:(4 + 2 * n) * AW].rearrange("p (c n) -> p c n", c=DC) for n in (0, 1)]
        vp = [acts[:, (6 + 2 * n) * AW:(8 + 2 * n) * AW].rearrange("p (c n) -> p c n", c=KT) for n in (0, 1)]
        pr0 = 10 * AW
        probs = [[acts[:, pr0 + (2 * s + n) * NT:pr0 + (2 * s + n + 1) * NT] for n in (0, 1)] for s in range(PROBS)]
        z2_hi, z2_lo = qp
        hid = [acts[:, 2 * AW + n * HC * NT:2 * AW + (n + 1) * HC * NT].rearrange("p (c n) -> p c n", c=HC)
               for n in (0, 1)]

        raw = sb("raw", [P, 2, NT])
        x_in = sb("x_in", [P, SLABS, P])
        x_res = sb("x_res", [P, TILES, D])
        mask = sb("mask", [P, 2, NT])
        staged = sb("staged", [P, BANKS, NT])
        bv = sb("bv", [P, D])
        bqk = sb("bqk", [P, 2, DC])
        small = sb("small", [P, 3 * HC + 9])
        w_max = small[:, 0:3 * HC]
        eps, gates, tg, tg_ffn, w_top, large = (small[:, 3 * HC + n:3 * HC + m] for n, m in
                                                ((0, 1), (1, 3), (3, 5), (5, 6), (6, 8), (8, 9)))
        large = large.bitcast(i32)
        bn = sb("bn", [P, QUADS, SLABS, 6])
        mv = sb("mv", [P, SLABS, 2])

        bank = [es.enter_context(nc.psum_tensor(f"bank{n}", [P, NT], f32)) for n in range(BANKS)]
        acc = [es.enter_context(nc.psum_tensor(f"acc{n}", [P, D], f32)) for n in range(TILES)]

        carrier = sem("carrier")
        gates_loaded = sem("gates_loaded")
        biases_loaded = sem("biases_loaded")
        w_loaded = [sem(f"w_loaded{n}") for n in range(3 * DC)]
        first_loaded = [sem(f"first_loaded{n}") for n in range(DC)]
        w_hi_done = sem("w_hi_done")
        wk_split, wvq_split = sem("wk_split"), sem("wvq_split")
        consts_set, consts_ready = sem("consts_set"), sem("consts_ready")
        raw_loaded = [sem(f"raw_loaded{n}") for n in (0, 1)]
        ctx_in_mask = [sem(f"ctx_in_mask{n}") for n in (0, 1)]
        ctx_hi_done, ctx_split = sem("ctx_hi_done"), sem("ctx_split")
        x_loaded = [sem(f"x_loaded{n}") for n in range(QUADS)]
        bn_shared = sem("bn_shared")
        res_loaded = [sem(f"res_loaded{n}") for n in range(TILES)]
        stored = [sem(f"stored{n}") for n in range(TILES)]
        mask_loaded = [sem(f"mask_loaded{n}") for n in (0, 1)]
        bn_done, mv_done, std_done, rstd_done = (sem(n) for n in ("bn_done", "mv_done", "std_done", "rstd_done"))
        z_ready, z_turned = sem("z_ready"), sem("z_turned")
        z_hi_done, z_split = sem("z_hi_done"), sem("z_split")
        group_ready = sem("group_ready")
        staged_act, staged_dve = sem("staged_act"), sem("staged_dve")
        hi_done = sem("hi_done")
        split_done = sem("split_done")
        acc_ready, relu_done = sem("acc_ready"), sem("relu_done")
        x2_ready = sem("x2_ready")
        ffn_cast = sem("ffn_cast")
        w_ranged, top_done, top_all, large_set = (sem(n) for n in ("w_ranged", "top_done", "top_all", "large_set"))
        lo_loaded = [sem(f"lo_loaded{n}") for n in (0, 1)]
        lo_split = sem("lo_split")
        ffn_ready = sem("ffn_ready")
        silu_done, hid_full, hid_hi_done, hid_split = (sem(n) for n in ("silu_done", "hid_full", "hid_hi_done", "hid_split"))
        down_ready, y_ready = sem("down_ready"), sem("y_ready")

        def done_at(b, name):
            return b * G + gid[name] + 1

        def split_at(b, name):
            return done_at(b, name) + BANKS

        def free_at(b, name):
            return done_at(b, name)

        EXACT = 4096.0
        down_lo = acts[:, 8 * AW:8 * AW + HC * D].rearrange("p (c n) -> p c n", c=HC)
        lo_slots = [operands[:, 9 * OPW + n * NT:9 * OPW + (n + 1) * NT].rearrange("p (c n) -> p c n", c=DC)
                    for n in range(4)]
        assert 2 * AW + 2 * HC * NT <= 8 * AW

        def lo_at(t, c, n):
            return HC + 2 * HC * t + 2 * c + n + 1

        ffn_plan = ({("v", 4 + t): n for t, n in enumerate((1, 1, 1, 1))}
                    | {("q", 1, e): n for e, n in enumerate((1, 1, 1, 2))}
                    | {("s", 0, k): n for k, n in enumerate((2, 2, 2, 2, 1, 1, 0, 2))}
                    | {("s", 1, k): n for k, n in enumerate((2, 2, 2, 2, 2, 2, 2, 1))})
        ffn_before, n = {}, 0
        for name in order:
            ffn_before[name] = range(n, n + ffn_plan.get(name, 0))
            n += ffn_plan.get(name, 0)
        assert n == 3 * HC

        def loads_until(name):
            return ffn_before[name].start + 2

        LAST = B - 1
        W_PIECES = 3 * DC
        FFN_PIECES = 3 * HC
        CTX_PIECES = UNITS * DC
        CTX_ALL = B * CTX_PIECES
        LN_A = B * UNITS

        def w_piece(n):
            w, c = (w_k, w_v, w_q)[n // DC], n % DC
            hi, lo = ((wk_hi, wk_lo), (wv_hi, wv_lo), (wq_hi, wq_lo))[n // DC]
            slot = (staged[:, c, :], x_res[:, c, :], first_slot(c))[n // DC]
            return w[c * P:(c + 1) * P, :], slot, hi[:, c, :], lo[:, c, :]

        def first_slot(c):
            return raw[:, c, :] if c < 2 else mask[:, c - 2, :]

        RAW_FILLS = DC // 2 + 1

        def ctx_slot(blk, c):
            return mask[:, c - 2, :] if blk == 1 and c >= 2 else raw[:, c % 2, :]

        def ctx_loaded(b, blk, c):
            if blk == 1 and c >= 2:
                return ctx_in_mask[c - 2], 16 * (b + 1)
            return raw_loaded[c % 2], 16 * (b * RAW_FILLS + (c // 2 if blk == 0 else DC // 2) + 1 - DC // 2)

        def ffn_piece(n):
            kind, m = divmod(n, HC)
            if kind < 2:
                c, h = divmod(m, H // NT)
                src = (wg_t, wu_t)[kind][c * P:(c + 1) * P, h * NT:(h + 1) * NT]
                return src, (ffn_gate, ffn_up)[kind][:, c, h * NT:(h + 1) * NT]
            return wd_t[m * P:(m + 1) * P, :], ffn_down[:, m, :]

        ctx_before = ((0, 1), (2,), (3,), ())
        turned_after = ({4: (0,), 5: (1, 2), 6: (3,)}, {5: (0,), 6: (1,), 7: (2, 3)})
        split_after = ({5: (0,), 6: (1, 2, 3)}, {6: (0,), 7: (1, 2, 3)})

        def turned(j):
            return x_in[:, j * SLABS_T:(j + 1) * SLABS_T, :].rearrange("p m (c j) -> p c m j", c=DC)

        def squares(z, j):
            return z[:, :, j * P:(j + 1) * P].rearrange("p c (m j) -> p c m j", j=SQ)

        block = es.enter_context(nc.Block())

        @block.sync
        def _(sp):
            def sp_wait(semaphore, value):
                sp.wait_ge(semaphore, value)
                sp.sem_inc(carrier, 1)

            def load_w(n):
                src, slot, _, _ = w_piece(n)
                sp.dma_start(slot, src).then_inc(w_loaded[n], 16)

            def load_ctx(b, blk, c):
                if blk == 1 and c >= 2:
                    sp_wait(split_done, split_at(b, ("k", 0, 0)))
                elif blk == 1:
                    sp_wait(ctx_split, b * CTX_PIECES + c + 3)
                elif c < 2:
                    sp_wait(ctx_split, b * CTX_PIECES + c - 3)
                else:
                    sp_wait(ctx_split, b * CTX_PIECES + c - 1)
                sp.dma_start(ctx_slot(blk, c), ctx_t[b, c * P:(c + 1) * P, blk * NT:(blk + 1) * NT]) \
                    .then_inc(ctx_loaded(b, blk, c)[0], 16)

            def load_rows(rows):
                for a in range(QUADS):
                    sp.dma_start(x_in[a * SQ:(a + 1) * SQ, :, :],
                                 rows[:, a * P:(a + 1) * P].rearrange("(m j) i -> j m i", j=SQ)).then_inc(x_loaded[a], 16)

            def share(ln):
                sp_wait(bn_done, TILES * (ln + 1))
                for r in range(1, QUADS):
                    n = P - r * SQ
                    sp.dma_start(bn[0:n, r, :, :], bn[P - n:P, 0, :, :]).then_inc(bn_shared, 16)
                    sp.dma_start(bn[n:P, r, :, :], bn[0:P - n, 0, :, :]).then_inc(bn_shared, 16)

            def load_res(b, u, j):
                r = u * NT + j * P
                sp.dma_start(x_res[:, j, :], x[b, r:r + P, :]).then_inc(res_loaded[j], 16)

            def store_x2(b, u):
                for j in range(TILES):
                    r = u * NT + j * P
                    sp_wait(x2_ready, TILES * (b * UNITS + u + 1) + j + 1)
                    sp.dma_start(x2[b, r:r + P, :], x_res[:, j, :]).then_inc(stored[j], 16)

            def load_ffn(n):
                if n < 2:
                    sp.wait_ge(ctx_split, CTX_ALL - DC + 1 + n)
                else:
                    sp.wait_ge(ffn_cast, n - 1)
                    sp.wait_ge(w_ranged, n - 1)
                sp.dma_start(raw[:, n % 2, :].bitcast(i32), ffn_piece(n)[0]).then_inc(raw_loaded[n % 2], 16)

            load_rows(x[0, 0:NT, :])
            for c in range(DC):
                load_w(c)
                sp.dma_start(first_slot(c), ctx_t[0, c * P:(c + 1) * P, 0:NT]).then_inc(first_loaded[c], 16)
            share(0)
            for c in range(DC):
                load_w(DC + c)
            for c in range(DC):
                sp.wait_ge(ctx_split, c + 1)
                load_w(2 * DC + c)
            sp.wait_ge(wvq_split, 2 * DC)
            for j in range(TILES):
                load_res(0, 0, j)

            def batch(b, last):
                for c in range(DC):
                    load_ctx(b, 1, c)
                sp_wait(z_split, TILES * (b * UNITS + 1))
                load_rows(x[b, NT:2 * NT, :])
                if last:
                    for n in range(loads_until(("s", 0, 2))):
                        load_ffn(n)
                share(b * UNITS + 1)
                if last:
                    for n in range(loads_until(("s", 0, 2)), loads_until(("s", 0, 7))):
                        load_ffn(n)
                sp_wait(z_split, TILES * (b * UNITS + 2))
                load_rows(x2[0, 0:NT, :] if last else x[b + 1, 0:NT, :])
                if last:
                    for n in range(loads_until(("s", 0, 7)), loads_until(("s", 1, 0))):
                        load_ffn(n)
                else:
                    for c in range(2):
                        load_ctx(b + 1, 0, c)
                store_x2(b, 0)
                for j in range(TILES):
                    sp_wait(stored[j], 16 * (b * UNITS + 1))
                    load_res(b, 1, j)
                if last:
                    for n in range(loads_until(("s", 1, 0)), loads_until(("s", 1, 2))):
                        load_ffn(n)
                else:
                    load_ctx(b + 1, 0, 2)
                share((b + 1) * UNITS)
                if last:
                    for n in range(loads_until(("s", 1, 2)), FFN_PIECES):
                        load_ffn(n)
                else:
                    load_ctx(b + 1, 0, 3)
                store_x2(b, 1)
                if not last:
                    for j in range(TILES):
                        sp_wait(stored[j], 16 * (b * UNITS + 2))
                        load_res(b + 1, 0, j)

            with sp.Fori(0, LAST) as b:
                batch(b, False)
            batch(LAST, True)

            for j in range(TILES):
                sp.wait_ge(stored[j], 16 * BLOCKS)
            x2_rows = x2.rearrange("b (t n) d -> (b t) n d", n=NT)
            out_rows = out.rearrange("b (t n) d -> (b t) n d", n=NT)

            def ffn_block(t, last, general):
                if not last:
                    sp_wait(z_split, TILES * (LN_A + t + 1))
                    load_rows(x2_rows[t + 1, :, :])
                for j in range(TILES):
                    sp_wait(stored[j], 16 * (BLOCKS + t))
                    sp.dma_start(x_res[:, j, :], x2_rows[t, j * P:(j + 1) * P, :]).then_inc(res_loaded[j], 16)
                if general:
                    for c in range(HC):
                        for n, w in enumerate((wg_t, wu_t)):
                            sp_wait(lo_split, lo_at(t, c, n) - 2)
                            sp.dma_start(raw[:, n, :].bitcast(i32).rearrange("p (c n) -> p c n", c=DC),
                                         w[:, c * P:(c + 1) * P].rearrange("(c p) n -> p c n", p=P)) \
                                .then_inc(lo_loaded[n], 16)
                        if c == 6 and not last:
                            share(LN_A + t + 1)
                elif not last:
                    share(LN_A + t + 1)
                for j in range(TILES):
                    sp_wait(y_ready, TILES * t + j + 1)
                    sp.dma_start(out_rows[t, j * P:(j + 1) * P, :], x_res[:, j, :]).then_inc(stored[j], 16)

            def load_down_lo():
                for c in range(HC):
                    if c < 2:
                        sp.wait_ge(w_ranged, FFN_PIECES)
                        sp.wait_ge(ffn_cast, FFN_PIECES)
                    else:
                        sp.wait_ge(lo_split, c - 1)
                    sp.dma_start(raw[:, c % 2, :].bitcast(i32), wd_t[c * P:(c + 1) * P, :]).then_inc(lo_loaded[c % 2], 16)

            def ffn(general):
                if general:
                    load_down_lo()
                with sp.Fori(0, BLOCKS - 1) as t:
                    ffn_block(t, False, general)
                ffn_block(BLOCKS - 1, True, general)

            sp.wait_ge(large_set, 1)
            with sp.If(sp.value_load(large[0:1, 0:1], min_val=0, max_val=1) == 1):
                ffn(True)
            with sp.Else():
                ffn(False)
            for j in range(TILES):
                sp.wait_ge(stored[j], 16 * 2 * BLOCKS)

        @block.gpsimd
        def _(pool):
            pool.dma_start(gates[:, 0:1], g_xattn.rearrange("(a n) -> a n", a=1).to_broadcast([P, 1])) \
                .then_inc(gates_loaded, 16)
            pool.dma_start(gates[:, 1:2], g_ffn.rearrange("(a n) -> a n", a=1).to_broadcast([P, 1])) \
                .then_inc(gates_loaded, 16)
            pool.dma_start(bqk[:, 0, :], b_q).then_inc(biases_loaded, 16)
            pool.dma_start(bqk[:, 1, :], b_k).then_inc(biases_loaded, 16)
            pool.dma_start(bv[:, :], b_v.rearrange("(a n) -> a n", a=1).to_broadcast([P, D])).then_inc(biases_loaded, 16)
            for c in range(DC):
                pool.wait_ge(ctx_hi_done, c + 1)
                pool.tensor_tensor(ctx_lo[:, c, :], first_slot(c), ctx_hi[:, c, :].bitcast(f32), ALU.subtract) \
                    .then_inc(ctx_split, 1)
            for n in range(DC, W_PIECES):
                _, slot, hi, lo = w_piece(n)
                pool.wait_ge(w_hi_done, n + 1)
                pool.tensor_tensor(lo, slot, hi.bitcast(f32), ALU.subtract).then_inc(wvq_split, 1)
            with pool.Fori(0, B) as b:
                for m in range(UNITS * KT):
                    u, k = divmod(m, KT)
                    if m < 2:
                        pool.wait_ge(ctx_split, (b + 1) * CTX_PIECES)
                    else:
                        pool.wait_ge(staged_dve, b * NV + vid["s", (m - 2) // KT, (m - 2) % KT] + 1)
                    pool.sem_inc(carrier, 1)
                    pool.dma_start(mask[:, m % 2, :], mask_t[k * P:(k + 1) * P, u * NT:(u + 1) * NT]) \
                        .then_inc(mask_loaded[m % 2], 16)
            pool.wait_ge(top_done, 1)
            pool.partition_all_reduce(w_top[:, 1:2], w_top[:, 0:1], P, RMAX).then_inc(top_all, 1)

        @block.scalar
        def _(act):
            act.wait_ge(gates_loaded, 16 * 2)
            nc.scalar.activation(tg[:, :], gates[:, :], ACT.Tanh).then_inc(consts_ready, 1)

            def w_hi(n):
                _, slot, hi, _ = w_piece(n)
                act.wait_ge(w_loaded[n], 16)
                nc.scalar.activation(hi, slot, ACT.Copy).then_inc(w_hi_done, 1)

            def ctx_part(b, blk, c):
                act.wait_ge(*ctx_loaded(b, blk, c))
                nc.scalar.activation(ctx_hi[:, c, :], ctx_slot(blk, c), ACT.Copy).then_inc(ctx_hi_done, 1)

            def ffn_weights(n):
                act.wait_ge(raw_loaded[n % 2], 16 * (B * RAW_FILLS - DC // 2 + n // 2 + 1))
                nc.scalar.activation(ffn_piece(n)[1], raw[:, n % 2, :].bitcast(i32), ACT.Copy).then_inc(ffn_cast, 1)

            def project(b, name):
                g = gid[name]
                kind, blk, e = name
                act.wait_ge(group_ready, done_at(b, name))
                act.wait_ge(split_done, free_at(b, name))
                bias, scale = (bqk[:, 0, e:e + 1], SCORE_SCALE) if kind == "q" else (bqk[:, 1, e:e + 1], 1.0)
                nc.scalar.activation(staged[:, g % BANKS, :], bank[g % BANKS][:, :], ACT.Relu, bias=bias,
                                     scale=scale).then_inc(staged_act, 1)
                act.wait_ge(staged_act, b * NA + aid[name] + 1)
                dst = qp[0][:, e, :] if kind == "q" else kp[0][:, e, blk * NT:(blk + 1) * NT]
                nc.scalar.activation(dst, staged[:, g % BANKS, :], ACT.Copy).then_inc(hi_done, 1)

            def value(b, name):
                g = gid[name]
                act.wait_ge(staged_dve, b * NV + vid[name] + 1)
                nc.scalar.activation(vp[0][:, name[1], :], staged[:, g % BANKS, :], ACT.Relu).then_inc(hi_done, 1)

            def logits(b, name):
                g = gid[name]
                act.wait_ge(staged_dve, b * NV + vid[name] + 1)
                nc.scalar.activation(probs[name[2] % PROBS][0], staged[:, g % BANKS, :], ACT.Copy).then_inc(hi_done, 1)

            def z_part(ln, j, hi):
                act.wait_ge(z_turned, TILES * ln + j + 1)
                nc.scalar.activation(squares(hi, j), turned(j), ACT.Copy).then_inc(z_hi_done, 1)

            def square_root(ln):
                act.wait_ge(mv_done, 2 * (ln + 1))
                nc.scalar.activation(mv[:, :, 1], mv[:, :, 1], ACT.Sqrt, bias=eps[:, 0:1]).then_inc(std_done, 1)

            def attended(b, u):
                for j in range(TILES):
                    act.wait_ge(acc_ready, TILES * (b * UNITS + u) + j + 1)
                    nc.scalar.activation(acc[j][:, :], acc[j][:, :], ACT.Relu).then_inc(relu_done, 1)

            act.wait_ge(consts_set, 1)
            for c in range(DC):
                w_hi(c)
                act.wait_ge(first_loaded[c], 16)
                nc.scalar.activation(ctx_hi[:, c, :], first_slot(c), ACT.Copy).then_inc(ctx_hi_done, 1)
            square_root(0)
            for n in range(DC, 2 * DC):
                w_hi(n)
            for j in range(TILES):
                z_part(0, j, z_hi)
            for n in range(2 * DC, W_PIECES):
                w_hi(n)
            act.wait_ge(biases_loaded, 16 * 3)
            nc.scalar.activation(bqk[:, 0, :], bqk[:, 0, :], ACT.Copy, scale=SCORE_SCALE).then_inc(consts_ready, 1)
            act.wait_ge(consts_ready, 2)
            act.wait_ge(wk_split, DC)

            def batch(b, last):
                for e in range(DC):
                    project(b, ("k", 0, e))
                for t in range(4):
                    value(b, ("v", t))
                for e in range(DC):
                    for c in ctx_before[e]:
                        ctx_part(b, 1, c)
                    project(b, ("q", 0, e))
                for e in range(DC):
                    project(b, ("k", 1, e))
                for t in range(4, 8):
                    if last:
                        for n in ffn_before["v", t]:
                            ffn_weights(n)
                    value(b, ("v", t))
                for k in range(KT):
                    if last:
                        for n in ffn_before["s", 0, k]:
                            ffn_weights(n)
                    logits(b, ("s", 0, k))
                    if k == 2:
                        square_root(b * UNITS + 1)
                    if k == 4:
                        act.wait_ge(group_ready, done_at(b, ("q", 0, DC - 1)))
                    for j in turned_after[0].get(k, ()):
                        z_part(b * UNITS + 1, j, z_hi)
                for e in range(DC):
                    if last:
                        for n in ffn_before["q", 1, e]:
                            ffn_weights(n)
                    project(b, ("q", 1, e))
                attended(b, 0)
                for k in range(KT):
                    if last:
                        for n in ffn_before["s", 1, k]:
                            ffn_weights(n)
                    logits(b, ("s", 1, k))
                    if k == 2:
                        square_root((b + 1) * UNITS)
                    if not last and k < DC:
                        ctx_part(b + 1, 0, k)
                    if not last:
                        if k == 4:
                            act.wait_ge(group_ready, done_at(b, ("q", 1, DC - 1)))
                        for j in turned_after[1].get(k, ()):
                            z_part((b + 1) * UNITS, j, z_hi)
                if last:
                    act.wait_ge(group_ready, done_at(b, ("s", 1, KT - 1)))
                    for j in range(TILES):
                        z_part(LN_A, j, z2_hi)
                attended(b, 1)

            with act.Fori(0, LAST) as b:
                batch(b, False)
            batch(LAST, True)

            def ffn_block(t, last):
                base = 2 * HC * t
                for c in range(HC):
                    act.wait_ge(ffn_ready, base + 2 * c + 1)
                    if c >= BANKS:
                        act.wait_ge(hid_split, t * HC + c - BANKS + 1)
                    nc.scalar.activation(staged[:, c % BANKS, :], bank[2 * c % BANKS][:, :], ACT.Silu, scale=DEQUANT) \
                        .then_inc(silu_done, 1)
                    act.wait_ge(hid_full, t * HC + c + 1)
                    nc.scalar.activation(hid[0][:, c, :], staged[:, c % BANKS, :], ACT.Copy).then_inc(hid_hi_done, 1)
                    if not last and c == 9:
                        square_root(LN_A + 1 + t)
                if not last:
                    act.wait_ge(ffn_ready, base + 2 * HC)
                    for j in range(TILES):
                        z_part(LN_A + 1 + t, j, z2_hi)

            with act.Fori(0, BLOCKS - 1) as t:
                ffn_block(t, False)
            ffn_block(BLOCKS - 1, True)

        @block.vector
        def _(dve):
            nc.vector.memset(eps[:, :], EPS).then_inc(consts_set, 1)
            dve.sem_inc(x2_ready, TILES)
            dve.sem_inc(split_done, BANKS)

            def w_lo(n):
                _, slot, hi, lo = w_piece(n)
                dve.wait_ge(w_hi_done, n + 1)
                nc.vector.tensor_tensor(lo, slot, hi.bitcast(f32), ALU.subtract).then_inc(wk_split, 1)

            def ctx_part(b, blk, c):
                n = blk * DC + c
                dve.wait_ge(ctx_hi_done, b * CTX_PIECES + n + 1)
                nc.vector.tensor_tensor(ctx_lo[:, c, :], ctx_slot(blk, c), ctx_hi[:, c, :].bitcast(f32), ALU.subtract) \
                    .then_inc(ctx_split, 1)

            def statistics(ln, j):
                if j == 0:
                    for a in range(QUADS):
                        dve.wait_ge(x_loaded[a], 16 * (ln + 1))
                for m in range(j * SLABS_T, (j + 1) * SLABS_T):
                    last_bn = nc.vector.bn_stats(bn[:, 0, m, :], x_in[:, m, :])
                last_bn.then_inc(bn_done, 1)

            def combine(ln, half):
                if half == 0:
                    dve.wait_ge(bn_shared, 16 * 2 * (QUADS - 1) * (ln + 1))
                    dve.sem_inc(carrier, 1)
                for m in range(half * SLABS // 2, (half + 1) * SLABS // 2):
                    last_mv = nc.vector.bn_aggr(mv[:, m, :], bn[:, :, m, :])
                last_mv.then_inc(mv_done, 1)

            def inverse(ln):
                dve.wait_ge(std_done, ln + 1)
                nc.vector.reciprocal(mv[:, :, 1], mv[:, :, 1]).then_inc(rstd_done, 1)
                dve.wait_ge(rstd_done, ln + 1)

            def normalise(j):
                for m in range(j * SLABS_T, (j + 1) * SLABS_T):
                    last_z = nc.vector.tensor_scalar(x_in[:, m, :], x_in[:, m, :], mv[:, m, 0:1], mv[:, m, 1:2],
                                                     ALU.subtract, ALU.mult)
                last_z.then_inc(z_ready, 1)

            def turn(ln, j):
                dve.wait_ge(z_ready, TILES * ln + j + 1)
                rows = x_in[:, j * SLABS_T:(j + 1) * SLABS_T, :]
                nc.vector.transpose(rows, rows).then_inc(z_turned, 1)

            def z_part(ln, j, hi, lo):
                dve.wait_ge(z_hi_done, TILES * ln + j + 1)
                nc.vector.tensor_tensor(squares(lo, j), turned(j), squares(hi, j).bitcast(f32), ALU.subtract) \
                    .then_inc(z_split, 1)

            def lo_part(b, name, src, hi, lo):
                dve.wait_ge(hi_done, done_at(b, name))
                nc.vector.tensor_tensor(lo, src, hi.bitcast(f32), ALU.subtract).then_inc(split_done, 1)

            def project(b, name):
                kind, blk, e = name
                hi, lo = (a[:, e, :] if kind == "q" else a[:, e, blk * NT:(blk + 1) * NT] for a in (qp if kind == "q" else kp))
                lo_part(b, name, staged[:, gid[name] % BANKS, :], hi, lo)

            def value(b, name):
                g, t = gid[name], name[1]
                dve.wait_ge(group_ready, done_at(b, name))
                dve.wait_ge(split_done, free_at(b, name))
                nc.vector.tensor_tensor(staged[:, g % BANKS, :], bank[g % BANKS][:, :], bv[:, :], ALU.add) \
                    .then_inc(staged_dve, 1)
                dve.wait_ge(hi_done, done_at(b, name))
                nc.vector.scalar_tensor_tensor(out=vp[1][:, t, :], in0=staged[:, g % BANKS, :], scalar=0.0,
                                               in1=vp[0][:, t, :].bitcast(f32), op0=ALU.max, op1=ALU.subtract) \
                    .then_inc(split_done, 1)

            def logits(b, name):
                g, u, k = gid[name], name[1], name[2]
                m = u * KT + k
                dve.wait_ge(group_ready, done_at(b, name))
                dve.wait_ge(split_done, free_at(b, name))
                dve.wait_ge(mask_loaded[m % 2], 16 * (b * (UNITS * KT // 2) + m // 2 + 1))
                nc.vector.scalar_tensor_tensor(out=staged[:, g % BANKS, :], in0=bank[g % BANKS][:, :], scalar=0.0,
                                               in1=mask[:, m % 2, :], op0=ALU.max, op1=ALU.add).then_inc(staged_dve, 1)
                hi, lo = probs[k % PROBS]
                lo_part(b, name, staged[:, g % BANKS, :], hi, lo)

            def residual(b, u):
                for j in range(TILES):
                    dve.wait_ge(relu_done, TILES * (b * UNITS + u) + j + 1)
                    dve.wait_ge(res_loaded[j], 16 * (b * UNITS + u + 1))
                    nc.vector.scalar_tensor_tensor(out=x_res[:, j, :], in0=acc[j][:, :], scalar=tg[:, 0:1],
                                                   in1=x_res[:, j, :], op0=ALU.mult, op1=ALU.add).then_inc(x2_ready, 1)

            for j in range(TILES):
                statistics(0, j)
            for c in range(DC):
                w_lo(c)
            combine(0, 0)
            combine(0, 1)
            inverse(0)
            for j in range(TILES):
                normalise(j)
            for j in range(TILES):
                turn(0, j)
            for j in range(TILES):
                z_part(0, j, z_hi, z_lo)
            dve.wait_ge(consts_ready, 2)
            nc.vector.tensor_scalar(tg_ffn[:, :], tg[:, 1:2], DEQUANT, DEQUANT, ALU.mult, ALU.mult).then_inc(consts_set, 1)

            def batch(b, last):
                for e in range(DC):
                    project(b, ("k", 0, e))
                for t in range(4):
                    value(b, ("v", t))
                for e in range(DC):
                    for c in ctx_before[e]:
                        ctx_part(b, 1, c)
                    project(b, ("q", 0, e))
                for e in range(DC):
                    project(b, ("k", 1, e))
                for t in range(4, 8):
                    if last:
                        for n in ffn_before["v", t]:
                            ranged(n)
                    value(b, ("v", t))
                for k in range(KT):
                    if last:
                        for n in ffn_before["s", 0, k]:
                            ranged(n)
                    logits(b, ("s", 0, k))
                    norm_step(b * UNITS + 1, k, 0)
                    for j in split_after[0].get(k, ()):
                        z_part(b * UNITS + 1, j, z_hi, z_lo)
                for e in range(DC):
                    if last:
                        for n in ffn_before["q", 1, e]:
                            ranged(n)
                    project(b, ("q", 1, e))
                residual(b, 0)
                for k in range(KT):
                    if last:
                        for n in ffn_before["s", 1, k]:
                            ranged(n)
                        if k == KT - 1:
                            dve.wait_ge(w_ranged, FFN_PIECES)
                            nc.vector.tensor_reduce(w_top[:, 0:1], w_max[:, :], AX.X, ALU.max).then_inc(top_done, 1)
                    logits(b, ("s", 1, k))
                    norm_step((b + 1) * UNITS, k, 0 if last else 1)
                    if not last and k < DC:
                        ctx_part(b + 1, 0, k)
                    if not last:
                        for j in split_after[1].get(k, ()):
                            z_part((b + 1) * UNITS, j, z_hi, z_lo)
                if last:
                    dve.wait_ge(top_all, 1)
                    nc.vector.tensor_scalar(large[:, :], w_top[:, 1:2], EXACT, None, ALU.is_gt).then_inc(large_set, 1)
                    for j in range(TILES):
                        z_part(LN_A, j, z2_hi, z2_lo)
                residual(b, 1)

            def norm_step(ln, k, next_block):
                if k < 2:
                    statistics(ln, 2 * k)
                    statistics(ln, 2 * k + 1)
                if k == 2:
                    combine(ln, 0)
                    combine(ln, 1)
                if k == 3:
                    inverse(ln)
                if k in (3, 4):
                    normalise(2 * k - 6)
                    normalise(2 * k - 5)
                for j in turned_after[next_block].get(k, ()):
                    turn(ln, j)

            def ranged(n):
                dve.wait_ge(raw_loaded[n % 2], 16 * (B * RAW_FILLS - DC // 2 + n // 2 + 1))
                nc.vector.tensor_reduce(w_max[:, n:n + 1], raw[:, n % 2, :].bitcast(i32), AX.X, ALU.max,
                                        apply_absolute_value=True).then_inc(w_ranged, 1)

            with dve.Fori(0, LAST) as b:
                batch(b, False)
            batch(LAST, True)

            def result(t, j):
                dve.wait_ge(down_ready, TILES * t + j + 1)
                dve.wait_ge(res_loaded[j], 16 * (BLOCKS + t + 1))
                nc.vector.scalar_tensor_tensor(out=x_res[:, j, :], in0=acc[j][:, :], scalar=tg_ffn[:, 0:1],
                                               in1=x_res[:, j, :], op0=ALU.mult, op1=ALU.add).then_inc(y_ready, 1)

            def ffn_block(t, last, general):
                base = 2 * HC * t
                for c in range(HC):
                    if general:
                        for n, w in enumerate((ffn_gate, ffn_up)):
                            dve.wait_ge(lo_loaded[n], 16 * (HC // 2 + HC * t + c + 1))
                            dve.wait_ge(ffn_ready, base + (2 * c + n - 3 if c >= 2 else 0))
                            nc.vector.tensor_tensor(lo_slots[(2 * c + n) % 4],
                                                    raw[:, n, :].bitcast(i32).rearrange("p (c n) -> p c n", c=DC),
                                                    w[:, :, c * P:(c + 1) * P].bitcast(f32), ALU.subtract) \
                                .then_inc(lo_split, 1)
                    dve.wait_ge(ffn_ready, base + 2 * c + 2)
                    dve.wait_ge(silu_done, t * HC + c + 1)
                    s = staged[:, c % BANKS, :]
                    nc.vector.tensor_tensor(s, bank[(2 * c + 1) % BANKS][:, :], s, ALU.mult).then_inc(hid_full, 1)
                    dve.wait_ge(hid_hi_done, t * HC + c + 1)
                    nc.vector.tensor_tensor(hid[1][:, c, :], s, hid[0][:, c, :].bitcast(f32), ALU.subtract) \
                        .then_inc(hid_split, 1)
                    if not last:
                        ln = LN_A + 1 + t
                        if 2 <= c < 6:
                            statistics(ln, c - 2)
                        if c in (7, 8):
                            combine(ln, c - 7)
                        if c == 10:
                            inverse(ln)
                            normalise(0)
                if not last:
                    for j in range(1, TILES):
                        normalise(j)
                    for j in range(TILES):
                        turn(ln, j)
                    for j in range(TILES):
                        z_part(ln, j, z2_hi, z2_lo)
                for j in range(TILES):
                    result(t, j)

            def ffn(general):
                if general:
                    dve.wait_ge(acc_ready, TILES * BLOCKS)
                    for c in range(HC):
                        dve.wait_ge(lo_loaded[c % 2], 16 * (c // 2 + 1))
                        nc.vector.tensor_tensor(down_lo[:, c, :], raw[:, c % 2, :].bitcast(i32),
                                                ffn_down[:, c, :].bitcast(f32), ALU.subtract).then_inc(lo_split, 1)
                with dve.Fori(0, BLOCKS - 1) as t:
                    ffn_block(t, False, general)
                ffn_block(BLOCKS - 1, True, general)

            dve.wait_ge(large_set, 1)
            with dve.If(dve.value_load(large[0:1, 0:1], min_val=0, max_val=1) == 1):
                ffn(True)
            with dve.Else():
                ffn(False)

        @block.tensor
        def _(pe):
            mm = nc.tensor.matmul

            def three_pass(dst, pairs, first=True, final=True):
                n, out = 3 * len(pairs), None
                terms = [t for lh, ll, rh, rl in pairs for t in ((lh, rh), (lh, rl), (ll, rh))]
                for i, (left, right) in enumerate(terms):
                    out = mm(dst, left, right, start=(first and i == 0), stop=(final and i == n - 1))
                return out

            def keys(b, blk, e):
                name = ("k", blk, e)
                pe.wait_ge(split_done, free_at(b, name))
                cols = slice(e * P, (e + 1) * P)
                three_pass(bank[gid[name] % BANKS][:, :],
                           [(wk_hi[:, c, cols], wk_lo[:, c, cols], ctx_hi[:, c, :], ctx_lo[:, c, :]) for c in range(DC)]) \
                    .then_inc(group_ready, 1)

            def queries(b, u, e):
                name = ("q", u, e)
                pe.wait_ge(split_done, free_at(b, name))
                cols = slice(e * P, (e + 1) * P)
                three_pass(bank[gid[name] % BANKS][:, :],
                           [(wq_hi[:, c, cols], wq_lo[:, c, cols], z_hi[:, c, :], z_lo[:, c, :]) for c in range(DC)]) \
                    .then_inc(group_ready, 1)

            def values(b, t):
                name = ("v", t)
                pe.wait_ge(split_done, free_at(b, name))
                cols = slice(t % TILES * P, (t % TILES + 1) * P)
                three_pass(bank[gid[name] % BANKS][:, :],
                           [(ctx_hi[:, c, cols], ctx_lo[:, c, cols], wv_hi[:, c, :], wv_lo[:, c, :]) for c in range(DC)]) \
                    .then_inc(group_ready, 1)

            def scores(b, u, k):
                name = ("s", u, k)
                pe.wait_ge(split_done, free_at(b, name))
                if k == 0:
                    pe.wait_ge(split_done, split_at(b, ("k", 1, DC - 1) if u == 0 else ("q", 1, DC - 1)))
                cols = slice(k * P, (k + 1) * P)
                three_pass(bank[gid[name] % BANKS][:, :],
                           [(kp[0][:, c, cols], kp[1][:, c, cols], qp[0][:, c, :], qp[1][:, c, :]) for c in range(DC)]) \
                    .then_inc(group_ready, 1)

            def attend(b, u, k):
                pe.wait_ge(split_done, split_at(b, ("s", u, k)))
                lh, ll = probs[k % PROBS]
                for j in range(TILES):
                    if k == 0:
                        pe.wait_ge(x2_ready, TILES * (b * UNITS + u) + j + 1)
                    cols = slice(j * P, (j + 1) * P)
                    last = three_pass(acc[j][:, :], [(lh[:, cols], ll[:, cols], vp[0][:, k, :], vp[1][:, k, :])],
                                      first=(k == 0), final=(k == KT - 1))
                    if k == KT - 1:
                        last.then_inc(acc_ready, 1)

            def batch(b, last):
                pe.wait_ge(wk_split, DC)
                pe.wait_ge(ctx_split, b * CTX_PIECES + DC)
                for e in range(DC):
                    keys(b, 0, e)
                pe.wait_ge(wvq_split, DC)
                for t in range(4):
                    values(b, t)
                pe.wait_ge(wvq_split, 2 * DC)
                pe.wait_ge(z_split, TILES * (b * UNITS + 1))
                for e in range(DC):
                    queries(b, 0, e)
                pe.wait_ge(ctx_split, b * CTX_PIECES + 2 * DC)
                for e in range(DC):
                    keys(b, 1, e)
                for t in range(4, 8):
                    values(b, t)
                for k in range(KT):
                    scores(b, 0, k)
                    if k >= LAG:
                        attend(b, 0, k - LAG)
                pe.wait_ge(z_split, TILES * (b * UNITS + 2))
                for e in range(DC):
                    queries(b, 1, e)
                for k in range(KT - LAG, KT):
                    attend(b, 0, k)
                for k in range(KT):
                    scores(b, 1, k)
                    if k >= LAG:
                        attend(b, 1, k - LAG)
                attend(b, 1, KT - 2)
                attend(b, 1, KT - 1)

            with pe.Fori(0, LAST) as b:
                batch(b, False)
            batch(LAST, True)

            pe.wait_ge(ffn_cast, FFN_PIECES)

            def ffn_block(t, last, general):
                pe.wait_ge(z_split, TILES * (LN_A + t + 1))
                for c in range(HC):
                    cols = slice(c * P, (c + 1) * P)
                    if c >= 2:
                        pe.wait_ge(hid_split, t * HC + c - 1)
                    for n, w in enumerate((ffn_gate, ffn_up)):
                        terms = [(w[:, i, cols], z[:, i, :]) for i in range(DC) for z in (z2_hi, z2_lo)]
                        if general:
                            pe.wait_ge(lo_split, lo_at(t, c, n))
                            terms += [(lo_slots[(2 * c + n) % 4][:, i, :], z2_hi[:, i, :]) for i in range(DC)]
                        for i, (left, right) in enumerate(terms):
                            last_mm = mm(bank[(2 * c + n) % BANKS][:, :], left, right, start=(i == 0),
                                         stop=(i == len(terms) - 1))
                        last_mm.then_inc(ffn_ready, 1)
                for j in range(TILES):
                    cols = slice(j * P, (j + 1) * P)
                    for c in range(HC):
                        if j == 0:
                            pe.wait_ge(hid_split, t * HC + c + 1)
                        terms = [(hid[0][:, c, cols], ffn_down[:, c, :]), (hid[1][:, c, cols], ffn_down[:, c, :])]
                        if general:
                            terms.append((hid[0][:, c, cols], down_lo[:, c, :]))
                        for i, (left, right) in enumerate(terms):
                            last_mm = mm(acc[j][:, :], left, right, start=(c == 0 and i == 0),
                                         stop=(c == HC - 1 and i == len(terms) - 1))
                    last_mm.then_inc(down_ready, 1)

            def ffn(general):
                with pe.Fori(0, BLOCKS - 1) as t:
                    ffn_block(t, False, general)
                ffn_block(BLOCKS - 1, True, general)

            pe.wait_ge(large_set, 1)
            with pe.If(pe.value_load(large[0:1, 0:1], min_val=0, max_val=1) == 1):
                ffn(True)
            with pe.Else():
                ffn(False)


def kernel(x, ctx_1024, mask_1xSxS2_ff0, g_xattn, g_ffn, L0_xattn_kernel_q, L0_xattn_kernel_k, L0_xattn_kernel_v,
           L0_xattn_bias_q, L0_xattn_bias_k, L0_xattn_bias_v, L0_ffn_w_gate, L0_ffn_w_up, L0_ffn_w_down):
    import concourse.bacc as bacc
    from concourse.bass_utils import run_bass_kernel_spmd

    D = x.shape[-1]

    def squares(w):
        return np.ascontiguousarray(w.reshape(4, 4, 32, -1).transpose(1, 0, 2, 3).reshape(D, -1))

    def columns(v):
        return np.ascontiguousarray(np.asarray(v).reshape(-1, 128).T)

    arrays = {
        "x": np.ascontiguousarray(x),
        "ctx_t": np.ascontiguousarray(np.asarray(ctx_1024).transpose(0, 2, 1)),
        "mask_t": np.ascontiguousarray(np.asarray(mask_1xSxS2_ff0)[0].T),
        "g_xattn": np.ascontiguousarray(g_xattn),
        "g_ffn": np.ascontiguousarray(g_ffn),
        "w_q": squares(np.asarray(L0_xattn_kernel_q).reshape(D, D)),
        "w_k": np.ascontiguousarray(np.asarray(L0_xattn_kernel_k).reshape(D, D)),
        "w_v": np.ascontiguousarray(np.asarray(L0_xattn_kernel_v).reshape(D, D)),
        "b_q": columns(L0_xattn_bias_q),
        "b_k": columns(L0_xattn_bias_k),
        "b_v": np.ascontiguousarray(L0_xattn_bias_v),
        "wg_t": squares(np.asarray(L0_ffn_w_gate).T),
        "wu_t": squares(np.asarray(L0_ffn_w_up).T),
        "wd_t": np.ascontiguousarray(np.asarray(L0_ffn_w_down).T),
    }
    nc = bacc.Bacc("TRN2", target_bir_lowering=False, num_devices=1)
    args = {name: nc.dram_tensor(f"{name}_dram", a.shape, mybir.dt.from_np(a.dtype), kind="ExternalInput").ap()
            for name, a in arrays.items()}
    out = nc.dram_tensor("out_dram", x.shape, mybir.dt.float32, kind="ExternalOutput").ap()
    x2 = nc.dram_tensor("x2_dram", x.shape, mybir.dt.float32, kind="Internal").ap()
    build(nc, *args.values(), out, x2)
    result = run_bass_kernel_spmd(nc, [{f"{name}_dram": a for name, a in arrays.items()}], core_ids=[0])
    return result.results[0]["out_dram"]
```
